# Optimizing a Trainium2 kernel written in Bass

```python
import numpy as np
import jax
import jax.numpy as jnp

def _softmax(x, axis=-1):
    return jax.nn.softmax(x, axis=axis)

def _gelu(x):
    return jax.nn.gelu(x, approximate=True)

def _silu(x):
    return jax.nn.silu(x)

def _sigmoid(x):
    return jax.nn.sigmoid(x)

def _layernorm(x, axis=-1, eps=1e-05):
    m = jnp.mean(x, axis=axis, keepdims=True)
    v = jnp.var(x, axis=axis, keepdims=True)
    return (x - m) / jnp.sqrt(v + eps)

def _scatter_add(tgt, idx, src, axis=0):
    return tgt.at[idx].add(src)

def _segment_sum(src, seg, n):
    return jax.ops.segment_sum(src, seg, n)
kernel_name = 'mk_macaron_d1_jaxref_r4_95fe4b'

def setup_inputs(seed: int=0):
    np.random.seed(seed)
    _w = jnp.asarray

    def _L0_attn_setup():
        import jax, jax.numpy as jnp
        import numpy as np
        import math
        D = 256
        H = 16
        DH = D // H

        def sinusoidal_pe(length, d):
            pos = jnp.arange(length, dtype=jnp.float32)[:, None]
            div = jnp.exp(jnp.arange(0, d, 2, dtype=jnp.float32) * (-math.log(10000.0) / d))
            ang = pos * div
            return jnp.stack([jnp.sin(ang), jnp.cos(ang)], axis=-1).reshape(length, d)

        def _relative_shift(pos_score):
            B, Hh, S1, S2 = pos_score.shape
            padded = jnp.concatenate([jnp.zeros((B, Hh, S1, 1), pos_score.dtype), pos_score], axis=-1)
            padded = padded.reshape(B, Hh, S2 + 1, S1)
            return padded[:, :, 1:].reshape(B, Hh, S1, S2)
        key = jax.random.key(seed)
        ks = jax.random.split(key, 12)
        s = 0.02
        x = jax.random.normal(ks[0], (2, 512, D), dtype=jnp.float32)
        return {'x': x, 'ln_g': jnp.ones((D,), jnp.float32), 'ln_b': jnp.zeros((D,), jnp.float32), 'Wq': jax.random.normal(ks[1], (D, D), jnp.float32) * s, 'bq': jnp.zeros((D,), jnp.float32), 'Wk': jax.random.normal(ks[2], (D, D), jnp.float32) * s, 'bk': jnp.zeros((D,), jnp.float32), 'Wv': jax.random.normal(ks[3], (D, D), jnp.float32) * s, 'bv': jnp.zeros((D,), jnp.float32), 'Wp': jax.random.normal(ks[4], (D, D), jnp.float32) * s, 'Wo': jax.random.normal(ks[5], (D, D), jnp.float32) * s, 'bo': jnp.zeros((D,), jnp.float32), 'u_bias': jax.random.normal(ks[6], (H, DH), jnp.float32) * 0.05, 'v_bias': jax.random.normal(ks[7], (H, DH), jnp.float32) * 0.05}
    _L0_attn_in = _L0_attn_setup()

    def _L0_ffn_setup():
        import jax, jax.numpy as jnp
        import numpy as np
        D_MODEL = 256
        key = jax.random.key(seed)
        k_x, k_w, k_a1, k_a2 = jax.random.split(key, 4)
        x = jax.random.normal(k_x, (4, 512, D_MODEL), dtype=jnp.float32)
        weight = jax.random.normal(k_w, (D_MODEL, D_MODEL), dtype=jnp.float32) * 0.02
        aux_weight1 = jax.random.normal(k_a1, (D_MODEL, D_MODEL), dtype=jnp.float32) * 0.02
        aux_weight2 = jax.random.normal(k_a2, (D_MODEL, D_MODEL), dtype=jnp.float32) * 0.02
        bias = jnp.zeros((D_MODEL,), dtype=jnp.float32)
        return {'x': x, 'weight': weight, 'aux_weight1': aux_weight1, 'aux_weight2': aux_weight2, 'bias': bias}
    _L0_ffn_in = _L0_ffn_setup()
    _d = {'L0_attn_x': _L0_attn_in['x'], 'L0_attn_ln_g': _L0_attn_in['ln_g'], 'L0_attn_ln_b': _L0_attn_in['ln_b'], 'L0_attn_Wq': _L0_attn_in['Wq'], 'L0_attn_bq': _L0_attn_in['bq'], 'L0_attn_Wk': _L0_attn_in['Wk'], 'L0_attn_bk': _L0_attn_in['bk'], 'L0_attn_Wv': _L0_attn_in['Wv'], 'L0_attn_bv': _L0_attn_in['bv'], 'L0_attn_Wp': _L0_attn_in['Wp'], 'L0_attn_Wo': _L0_attn_in['Wo'], 'L0_attn_bo': _L0_attn_in['bo'], 'L0_attn_u_bias': _L0_attn_in['u_bias'], 'L0_attn_v_bias': _L0_attn_in['v_bias'], 'L0_ffn_weight': _L0_ffn_in['weight'], 'L0_ffn_aux_weight1': _L0_ffn_in['aux_weight1'], 'L0_ffn_aux_weight2': _L0_ffn_in['aux_weight2'], 'L0_ffn_bias': _L0_ffn_in['bias']}
    _x0 = _d['L0_attn_x']
    _d['L0_attn_x'] = jax.random.normal(jax.random.fold_in(jax.random.key(seed), 1), (8, 1024, 256), dtype=_x0.dtype)
    del _x0
    return _d

def reference(L0_attn_x, L0_attn_ln_g, L0_attn_ln_b, L0_attn_Wq, L0_attn_bq, L0_attn_Wk, L0_attn_bk, L0_attn_Wv, L0_attn_bv, L0_attn_Wp, L0_attn_Wo, L0_attn_bo, L0_attn_u_bias, L0_attn_v_bias, L0_ffn_weight, L0_ffn_aux_weight1, L0_ffn_aux_weight2, L0_ffn_bias):

    def _L0_attn_ref(x, ln_g, ln_b, Wq, bq, Wk, bk, Wv, bv, Wp, Wo, bo, u_bias, v_bias):
        import jax, jax.numpy as jnp
        import numpy as np
        import math
        D = 256
        H = 16
        DH = D // H

        def sinusoidal_pe(length, d):
            pos = jnp.arange(length, dtype=jnp.float32)[:, None]
            div = jnp.exp(jnp.arange(0, d, 2, dtype=jnp.float32) * (-math.log(10000.0) / d))
            ang = pos * div
            return jnp.stack([jnp.sin(ang), jnp.cos(ang)], axis=-1).reshape(length, d)

        def _relative_shift(pos_score):
            B, Hh, S1, S2 = pos_score.shape
            padded = jnp.concatenate([jnp.zeros((B, Hh, S1, 1), pos_score.dtype), pos_score], axis=-1)
            padded = padded.reshape(B, Hh, S2 + 1, S1)
            return padded[:, :, 1:].reshape(B, Hh, S1, S2)
        B, S, Dm = x.shape
        dh = Dm // H
        scale = dh ** (-0.5)
        pe = sinusoidal_pe(S, Dm)
        mu = jnp.mean(x, axis=-1, keepdims=True)
        var = jnp.var(x, axis=-1, keepdims=True)
        xn = (x - mu) / jnp.sqrt(var + 1e-05) * ln_g + ln_b
        q = (xn @ Wq + bq).reshape(B, S, H, dh)
        k = (xn @ Wk + bk).reshape(B, S, H, dh)
        v = (xn @ Wv + bv).reshape(B, S, H, dh)
        p = (pe @ Wp).reshape(S, H, dh)
        content = jnp.einsum('bihd,bjhd->bhij', q + u_bias, k)
        pos = jnp.einsum('bihd,jhd->bhij', q + v_bias, p)
        pos = _relative_shift(pos)
        attn = jax.nn.softmax((content + pos) * scale, axis=-1)
        head = jnp.einsum('bhij,bjhd->bihd', attn, v).reshape(B, S, Dm)
        return head @ Wo + bo

    def _L0_ffn_ref(x, weight, aux_weight1, aux_weight2, bias):
        import jax, jax.numpy as jnp
        import numpy as np
        D_MODEL = 256
        h = jnp.einsum('btc,cd->btd', x, weight)
        h = jnp.einsum('btc,cd->btd', h, aux_weight1)
        h = jnp.einsum('btc,cd->btd', h, aux_weight2)
        return jnp.tanh(h + bias)
    x = L0_attn_x
    x = x + 0.5 * _L0_ffn_ref(_layernorm(x, axis=-1), L0_ffn_weight, L0_ffn_aux_weight1, L0_ffn_aux_weight2, L0_ffn_bias)
    x = x + _L0_attn_ref(_layernorm(x, axis=-1), L0_attn_ln_g, L0_attn_ln_b, L0_attn_Wq, L0_attn_bq, L0_attn_Wk, L0_attn_bk, L0_attn_Wv, L0_attn_bv, L0_attn_Wp, L0_attn_Wo, L0_attn_bo, L0_attn_u_bias, L0_attn_v_bias)
    x = x + 0.5 * _L0_ffn_ref(_layernorm(x, axis=-1), L0_ffn_weight, L0_ffn_aux_weight1, L0_ffn_aux_weight2, L0_ffn_bias)
    return x

_drawn_inputs = setup_inputs


def setup_inputs(seed=0):
    import zlib

    import numpy as np

    out = dict(_drawn_inputs(seed))
    spreads = {'L0_attn_ln_g': (1.0, 0.6),
     'L0_attn_ln_b': (0.0, 0.723),
     'L0_attn_bq': (0.0, 0.8),
     'L0_attn_bk': (0.0, 2.0),
     'L0_attn_bv': (0.0, 0.303),
     'L0_attn_bo': (0.0, 0.1),
     'L0_ffn_bias': (0.0, 0.1)}
    factors = {'L0_attn_Wq': 8.0,
     'L0_attn_Wk': 8.0,
     'L0_attn_Wv': 4.387,
     'L0_attn_Wp': 8.0,
     'L0_attn_u_bias': 8.0,
     'L0_attn_v_bias': 8.0}
    for name, (base, spread) in spreads.items():
        noise = np.random.default_rng([zlib.crc32(name.encode()), seed]).standard_normal(out[name].shape)
        drawn = base * np.exp(spread * noise) if base else spread * noise
        out[name] = jnp.asarray(drawn.astype(out[name].dtype))
    for name, factor in factors.items():
        out[name] = (out[name] * factor).astype(out[name].dtype)
    return out
```

```python
from contextlib import ExitStack

import concourse.bass as bass
from concourse import mybir

F32 = mybir.dt.float32
BF16 = mybir.dt.bfloat16
ALU = mybir.AluOpType
ACT = mybir.ActivationFunctionType

P = 128
B, S, D, H = 8, 1024, 256, 16
DH = D // H
C = D // P
EPS = 1e-5
SCALE = DH ** -0.5

LEFT_PARTS = [0, 0, 0, 1, 1, 2]
RIGHT_PARTS = [0, 1, 2, 0, 1, 0]
K6 = DH * len(LEFT_PARTS)

TILES = S // P
UNITS = H * B
NT = UNITS * TILES
BODY = 2 * TILES
LEAD = 6
READ_LAG = 3
RING = 4
PITCH = S + 1
QUAD = 4
VW = 32

GROUP = 4
ROWS = GROUP * P
GROUPS = B * S // ROWS


def at_once(eng, sem, value):
    eng.wait_ge(sem, value)
    eng.nop(nofuse=True)


def reused(eng, sem, value):
    if not isinstance(value, int) or value > 0:
        eng.wait_ge(sem, value)
        eng.nop(nofuse=True)


def over_rounds(eng, one):
    one(0)
    with eng.Fori(1, B) as b:
        one(b)


def broadcast_groups(row, n=GROUP):
    return row.unsqueeze(1).to_broadcast([P, n, D])


def layer_norm(eng, src, stats, moments, variance, scale, sems, at, out, twice):
    s_stats, s_moments, s_variance, s_scale, s_out = sems
    for t in range(GROUP):
        ins = eng.bn_stats(stats[:, t, :], src[:, t, :])
    ins.then_inc(s_stats, 1)
    at_once(eng, s_stats, at + 1)
    for t in range(GROUP):
        ins = eng.bn_aggr(moments[:, t, :], stats[:, t, :])
    ins.then_inc(s_moments, 1)
    eng.wait_ge(s_moments, at + 1)
    if twice:
        ins = eng.tensor_scalar(variance, moments[:, :, 1], 1.0 + EPS, EPS * EPS, ALU.mult, ALU.add)
    else:
        ins = eng.tensor_scalar(variance, moments[:, :, 1], EPS, None, ALU.add)
    ins.then_inc(s_variance, 1)
    eng.wait_ge(s_scale, at + 1)
    for t in range(GROUP):
        ins = eng.tensor_scalar(out[:, t, :], src[:, t, :], moments[:, t, 0:1], scale[:, t:t + 1],
                                ALU.subtract, ALU.mult)
    ins.then_inc(s_out, 1)


def inverse_root(pool, keep, variance, scale, sems, at):
    pool.wait_ge(sems[2], at + 1)
    pool.tensor_tensor(scale, variance, keep["minus_half"][:, :], ALU.pow).then_inc(sems[3], 1)


def turn_rows(eng, bank0, src, ident):
    for c in range(C):
        for t in range(GROUP):
            ins = eng.transpose(bank0[:, c, t * P:(t + 1) * P], src(t, c), ident[:, :])
    return ins


def rows_times(eng, banks, xT, w):
    for t in range(GROUP):
        for c in range(C):
            ins = eng.matmul(banks[:, t // 2, (t % 2) * D:(t % 2 + 1) * D],
                             xT[:, c, t * P:(t + 1) * P], w[:, c, :], start=(c == 0), stop=(c == C - 1))
    return ins


def setup_phase(nc, keep, a):
    with ExitStack() as ctx:
        def sb(name, shape, dt=F32):
            return ctx.enter_context(nc.sbuf_tensor("su_" + name, shape, dt))

        def sem(name):
            return ctx.enter_context(nc.semaphore("su_" + name))

        w_ffn, aux1, aux2, w_pos = (sb(n, [P, C, D]) for n in ("w_ffn", "aux1", "aux2", "w_pos"))
        pe_T = sb("pe_T", [P, C, S])
        turned = sb("turned", [P, 2, C, D])
        aux12 = sb("aux12", [P, C, D])
        ln_b_rep = sb("ln_b_rep", [P, C, P])
        cols = sb("cols", [P, 6, C])
        bv_row = sb("bv_row", [P, D])
        bq_k = sb("bq_k", [P, 2, C])
        pos = sb("pos", [P, C, S])
        parts = sb("parts", [P, 3, C, S], BF16)
        zeros = sb("zeros", [P, 2 * TILES])
        ps = ctx.enter_context(nc.psum_tensor("su_ps", [P, 8, 512], F32))
        loaded, pe_step, act_step, dve_step, stored = (
            sem(n) for n in ("loaded", "pe_step", "act_step", "dve_step", "stored"))
        LN_G, LN_B, BQ, BK, U, V = range(6)

        def chunks(x):
            return x.rearrange("(c p) n -> p c n", p=P)

        def by_feature(x):
            return x.rearrange("(c p) -> p c", p=P)

        loads = [
            (w_ffn[:, :, :], chunks(a["L0_ffn_weight"])), (aux1[:, :, :], chunks(a["L0_ffn_aux_weight1"])),
            (aux2[:, :, :], chunks(a["L0_ffn_aux_weight2"])), (w_pos[:, :, :], chunks(a["L0_attn_Wp"])),
            (keep["wq"][:, :, :], chunks(a["L0_attn_Wq"])), (keep["wk"][:, :, :], chunks(a["L0_attn_Wk"])),
            (keep["wv"][:, :, :], chunks(a["L0_attn_Wv"])), (keep["wo"][:, :, :], chunks(a["L0_attn_Wo"])),
            (pe_T[:, :, :], chunks(a["pe_T"])), (keep["ident"][:, :], a["ident"]), (keep["fold"][:, :], a["fold"]),
            (keep["b_ffn"][:, :], a["L0_ffn_bias"].partition_broadcast(P)),
            (keep["bo"][:, :], a["L0_attn_bo"].partition_broadcast(P)),
            (bv_row[:, :], a["L0_attn_bv"].partition_broadcast(P)),
        ]
        vectors = [(LN_G, a["L0_attn_ln_g"]), (LN_B, a["L0_attn_ln_b"]), (BQ, a["L0_attn_bq"]),
                   (BK, a["L0_attn_bk"]), (U, a["L0_attn_u_bias"].rearrange("h d -> (h d)")),
                   (V, a["L0_attn_v_bias"].rearrange("h d -> (h d)"))]
        n_loads = len(loads) + len(vectors)
        block = ctx.enter_context(nc.Block())

        @block.sync
        def _(sp):
            with nc.allow_non_contiguous_dma(reason="vectors of 256 by feature, and the zero column"):
                for dst, src in loads:
                    sp.dma_start(dst, src).then_inc(loaded, 16)
                for k, v in vectors:
                    sp.dma_start(cols[:, k, :], by_feature(v)).then_inc(loaded, 16)
                sp.wait_ge(dve_step, 1)
                sp.dma_start(a["scores"].rearrange("n (t p c) -> p (n t) c", p=P, c=PITCH)[:, :, 0], zeros[:, :])\
                    .then_inc(stored, 16)
            for k, need in enumerate((7, 9, 10)):
                sp.wait_ge(dve_step, need)
                sp.dma_start(a["pos_parts"][k].rearrange("(c p) m -> p c m", p=P), parts[:, k, :, :])\
                    .then_inc(stored, 16)
            sp.wait_ge(stored, 64)

        @block.tensor
        def _(pe):
            pe.wait_ge(loaded, 16 * n_loads)
            for k, w in enumerate((w_ffn, aux1)):
                for c in range(C):
                    for r in range(C):
                        ins = pe.transpose(ps[:, 2 * k + c, r * P:(r + 1) * P], w[:, r, c * P:(c + 1) * P],
                                           keep["ident"][:, :])
            ins.then_inc(pe_step, 1)
            for c in range(C):
                for n in range(2):
                    for k in range(C):
                        ins = pe.matmul(ps[:, 4 + 2 * c + n, :], w_pos[:, k, c * P:(c + 1) * P],
                                        pe_T[:, k, n * 512:(n + 1) * 512], start=(k == 0), stop=(k == C - 1))
            ins.then_inc(pe_step, 1)
            pe.wait_ge(act_step, 1)
            for r in range(C):
                for k in range(C):
                    ins = pe.matmul(ps[:, 0, r * D:(r + 1) * D], turned[:, 1, k, r * P:(r + 1) * P],
                                    aux2[:, k, :], start=(k == 0), stop=(k == C - 1))
            ins.then_inc(pe_step, 1)
            pe.wait_ge(dve_step, 2)
            for k in range(C):
                pe.matmul(ps[:, 1, 0:D], ln_b_rep[:, k, :], keep["wv"][:, k, :], start=(k == 0), stop=(k == C - 1))
            for i, w in enumerate(("wq", "wk")):
                for c in range(C):
                    for k in range(C):
                        ins = pe.matmul(ps[:, 2, 2 * i + c:2 * i + c + 1], keep[w][:, k, c * P:(c + 1) * P],
                                        cols[:, LN_B, k:k + 1], start=(k == 0), stop=(k == C - 1))
            ins.then_inc(pe_step, 1)
            pe.wait_ge(act_step, 2)
            for r in range(C):
                for k in range(C):
                    ins = pe.matmul(ps[:, 3, r * D:(r + 1) * D], turned[:, 0, k, r * P:(r + 1) * P],
                                    aux12[:, k, :], start=(k == 0), stop=(k == C - 1))
            ins.then_inc(pe_step, 1)

        @block.scalar
        def _(act):
            act.wait_ge(pe_step, 1)
            act.activation(turned[:, :, :, :].rearrange("p k c n -> p (k c) n"), ps[:, 0:4, 0:D], ACT.Copy)\
                .then_inc(act_step, 1)
            act.wait_ge(pe_step, 3)
            act.activation(aux12[:, :, :].rearrange("p c n -> p (c n)"), ps[:, 0, :], ACT.Copy).then_inc(act_step, 1)
            act.wait_ge(pe_step, 5)
            act.activation(keep["w3"][:, :, :].rearrange("p c n -> p (c n)"), ps[:, 3, :], ACT.Copy)\
                .then_inc(act_step, 1)

        @block.vector
        def _(dve):
            dve.memset(keep["minus_half"][:, :], -0.5)
            dve.memset(zeros[:, :], 0.0).then_inc(dve_step, 1)
            dve.wait_ge(loaded, 16 * n_loads)
            for c in range(C):
                ins = dve.tensor_copy(ln_b_rep[:, c, :], cols[:, LN_B, c:c + 1].to_broadcast([P, P]))
            ins.then_inc(dve_step, 1)
            dve.wait_ge(pe_step, 4)
            dve.tensor_tensor(keep["bv"][:, :], ps[:, 1, 0:D], bv_row[:, :], ALU.add)
            dve.tensor_tensor(bq_k[:, :, :].rearrange("p i c -> p (i c)"), ps[:, 2, 0:4],
                              cols[:, BQ:BK + 1, :].rearrange("p i c -> p (i c)"), ALU.add).then_inc(dve_step, 1)
            dve.wait_ge(dve_step, 3)
            dve.tensor_tensor(keep["b_qk"][:, 0, :], bq_k[:, 0, :], cols[:, U, :], ALU.add)
            dve.tensor_tensor(keep["b_qk"][:, 1, :], bq_k[:, 0, :], cols[:, V, :], ALU.add)
            dve.tensor_copy(keep["b_qk"][:, 2, :], bq_k[:, 1, :]).then_inc(dve_step, 1)
            for w in ("wq", "wk", "wv"):
                for c in range(C):
                    ins = dve.tensor_scalar(keep[w][:, c, :], keep[w][:, c, :], cols[:, LN_G, c:c + 1], None, ALU.mult)
            ins.then_inc(dve_step, 1)
            dve.wait_ge(pe_step, 2)
            dve.tensor_copy(pos[:, :, :].rearrange("p c m -> p (c m)"),
                            ps[:, 4:8, :].rearrange("p b m -> p (b m)")).then_inc(dve_step, 1)
            dve.wait_ge(dve_step, 6)
            dve.tensor_copy(parts[:, 0, :, :], pos[:, :, :]).then_inc(dve_step, 1)
            dve.wait_ge(dve_step, 7)
            dve.tensor_tensor(pos[:, :, :], pos[:, :, :], parts[:, 0, :, :], ALU.subtract).then_inc(dve_step, 1)
            dve.wait_ge(dve_step, 8)
            dve.tensor_copy(parts[:, 1, :, :], pos[:, :, :]).then_inc(dve_step, 1)
            dve.wait_ge(dve_step, 9)
            dve.tensor_tensor(parts[:, 2, :, :], pos[:, :, :], parts[:, 1, :, :], ALU.subtract).then_inc(dve_step, 1)


def dense_phase(nc, keep, a):
    with ExitStack() as ctx:
        def pair(name, shape, dt=F32):
            return [ctx.enter_context(nc.sbuf_tensor(f"de_{name}{k}", shape, dt)) for k in range(2)]

        def sem(name):
            return ctx.enter_context(nc.semaphore("de_" + name))

        x, x1, x1_bo, z, act_in = (pair(n, [P, GROUP, D]) for n in ("x", "x1", "x1_bo", "z", "act_in"))
        zT = pair("zT", [P, C, ROWS])
        stats, moments = pair("stats", [P, GROUP, 6]), pair("moments", [P, GROUP, 2])
        scale, variance = pair("scale", [P, GROUP]), pair("variance", [P, GROUP])
        qk = pair("qk", [P, 3, C, ROWS])
        parts = pair("parts", [P, 3, 3, C, ROWS], BF16)
        values = ctx.enter_context(nc.sbuf_tensor("de_values", [P, UNITS * P], F32))
        ps = [ctx.enter_context(nc.psum_tensor(f"de_ps{k}", [P, 4, 512], F32)) for k in range(2)]
        x_in = [sem(f"x_in{k}") for k in range(2)]
        x1_out = [sem(f"x1_out{k}") for k in range(2)]
        parts_out = [sem(f"parts_out{k}") for k in range(2)]
        ln1 = [sem("ln1_" + n) for n in ("stats", "moments", "variance", "scale", "out")]
        ln2 = [sem("ln2_" + n) for n in ("stats", "moments", "variance", "scale", "out")]
        (turned1, zT1, ffn, biased, tanhed, x1_ready, x1_bo_ready, turned2, zT2, qk_mm, q_copied, qk_copied,
         v_mm, v_copied, high, rest, mid, low, v_out) = (
            sem(n) for n in ("turned1", "zT1", "ffn", "biased", "tanhed", "x1_ready", "x1_bo_ready", "turned2",
                             "zT2", "qk_mm", "q_copied", "qk_copied", "v_mm", "v_copied", "high", "rest", "mid",
                             "low", "v_out"))
        rows = a["L0_attn_x"].rearrange("b (g t p) d -> p (b g) t d", p=P, t=GROUP)
        x1_rows = a["x1"].rearrange("(g t p) d -> p g t d", p=P, t=GROUP)
        qk_dram = a["qk_parts"]
        half = S // ROWS
        block = ctx.enter_context(nc.Block())

        @block.sync
        def _(sp):
            def load(b, k):
                sp.dma_start(x[k][:, :, :], rows[:, b * half + k, :, :]).then_inc(x_in[k], 16)

            for k in range(2):
                load(0, k)
            def one(b):
                for k in range(2):
                    g = b * 2 + k
                    sp.wait_ge(x1_bo_ready, g + 1)
                    sp.dma_start(x1_rows[:, g, :, :], x1_bo[k][:, :, :]).then_inc(x1_out[k], 16)
                    sp.wait_ge(low, g + 1)
                    for o in range(3):
                        for part in range(3):
                            dst = qk_dram[o, part, b, :, k * ROWS:(k + 1) * ROWS]
                            sp.dma_start(dst.rearrange("(c p) s -> p c s", p=P), parts[k][:, part, o, :, :])\
                                .then_inc(parts_out[k], 16)
                    sp.wait_ge(x1_ready, g + 1)
                    load((b + 1) % B, k)

            over_rounds(sp, one)
            sp.wait_ge(v_copied, GROUPS)
            sp.dma_start(a["values"].rearrange("u p n -> p u n"),
                         values[:, :].rearrange("p (u n) -> p u n", n=P)).then_inc(v_out, 16)
            for k in range(2):
                sp.wait_ge(x_in[k], 16 * (B + 1))
                sp.wait_ge(x1_out[k], 16 * B)
                sp.wait_ge(parts_out[k], 16 * 9 * B)
            sp.wait_ge(v_out, 16)

        @block.tensor
        def _(pe):
            def one(b):
                for k in range(2):
                    g = b * 2 + k
                    pe.wait_ge(ln1[4], g + 1)
                    reused(pe, v_copied, b * 2)
                    turn_rows(pe, ps[k], lambda t, c: z[k][:, t, c * P:(c + 1) * P], keep["ident"])\
                        .then_inc(turned1, 1)
                for k in range(2):
                    g = b * 2 + k
                    pe.wait_ge(zT1, g + 1)
                    reused(pe, qk_copied, b * 2)
                    rows_times(pe, ps[k][:, 2:4, :], zT[k], keep["w3"]).then_inc(ffn, 1)
                for k in range(2):
                    g = b * 2 + k
                    pe.wait_ge(ln2[4], g + 1)
                    turn_rows(pe, ps[k], lambda t, c: z[k][:, t, c * P:(c + 1) * P], keep["ident"])\
                        .then_inc(turned2, 1)
                for k in range(2):
                    g = b * 2 + k
                    pe.wait_ge(zT2, g + 1)
                    for i, w in enumerate(("wq", "wk")):
                        for c in range(C):
                            for kk in range(C):
                                ins = pe.matmul(ps[k][:, 2 * i + c, :], keep[w][:, kk, c * P:(c + 1) * P],
                                                zT[k][:, kk, :], start=(kk == 0), stop=(kk == C - 1))
                    ins.then_inc(qk_mm, 1)
                for k in range(2):
                    g = b * 2 + k
                    pe.wait_ge(q_copied, g + 1)
                    rows_times(pe, ps[k][:, 0:2, :], zT[k], keep["wv"]).then_inc(v_mm, 1)

            over_rounds(pe, one)

        @block.scalar
        def _(act):
            def one(b):
                for k in range(2):
                    g = b * 2 + k
                    act.wait_ge(turned1, g + 1)
                    reused(act, v_mm, b * 2)
                    act.activation(zT[k][:, :, :], ps[k][:, 0:2, :], ACT.Copy).then_inc(zT1, 1)
                for k in range(2):
                    g = b * 2 + k
                    act.wait_ge(biased, g + 1)
                    act.activation(act_in[k][:, :, :], act_in[k][:, :, :], ACT.Tanh).then_inc(tanhed, 1)
                for k in range(2):
                    g = b * 2 + k
                    act.wait_ge(turned2, g + 1)
                    act.activation(zT[k][:, :, :], ps[k][:, 0:2, :], ACT.Copy).then_inc(zT2, 1)
                for k in range(2):
                    g = b * 2 + k
                    act.wait_ge(qk_mm, g + 1)
                    reused(act, low, b * 2)
                    for o in range(3):
                        for c in range(C):
                            ins = act.activation(qk[k][:, o, c, :], ps[k][:, 2 * (o // 2) + c, :], ACT.Identity,
                                                 bias=keep["b_qk"][:, o, c:c + 1])
                        if o == 1:
                            ins.then_inc(q_copied, 1)
                    ins.then_inc(qk_copied, 1)

            over_rounds(act, one)

        @block.vector
        def _(dve):
            def one(b):
                for k in range(2):
                    g = b * 2 + k
                    dve.wait_ge(x_in[k], b * 16 + 16)
                    reused(dve, turned2, b * 2)
                    layer_norm(dve, x[k], stats[k], moments[k], variance[k][:, :], scale[k][:, :], ln1, g, z[k], False)
                for k in range(2):
                    g = b * 2 + k
                    dve.wait_ge(ffn, g + 1)
                    dve.tensor_tensor(act_in[k][:, :, :], ps[k][:, 2:4, :].rearrange("p a (t d) -> p (a t) d", d=D),
                                      broadcast_groups(keep["b_ffn"][:, :]), ALU.add).then_inc(biased, 1)
                for k in range(2):
                    g = b * 2 + k
                    dve.wait_ge(tanhed, g + 1)
                    reused(dve, x1_bo_ready, b * 2)
                    dve.scalar_tensor_tensor(x1[k][:, :, :].rearrange("p t d -> p (t d)"),
                                             act_in[k][:, :, :].rearrange("p t d -> p (t d)"), 0.5,
                                             x[k][:, :, :].rearrange("p t d -> p (t d)"), ALU.mult, ALU.add)\
                        .then_inc(x1_ready, 1)
                    dve.wait_ge(x1_ready, g + 1)
                    layer_norm(dve, x1[k], stats[k], moments[k], variance[k][:, :], scale[k][:, :], ln2, g, z[k],
                               True)
                for k in range(2):
                    g = b * 2 + k
                    dve.wait_ge(v_mm, g + 1)
                    dst = values[:, :].rearrange("p (h bt d) -> p bt h d", h=H, d=DH)
                    dve.tensor_tensor(dst[:, bass.ds(b * TILES + k * GROUP, GROUP), :, :],
                                      ps[k][:, 0:2, :].rearrange("p a (t h d) -> p (a t) h d", h=H, d=DH),
                                      broadcast_groups(keep["bv"][:, :]).rearrange("p t (h d) -> p t h d", d=DH),
                                      ALU.add).then_inc(v_copied, 1)
                for k in range(2):
                    g = b * 2 + k
                    flat = qk[k][:, :, :, :].rearrange("p o c s -> p (o c s)")
                    part = [parts[k][:, i, :, :, :].rearrange("p o c s -> p (o c s)") for i in range(3)]
                    dve.wait_ge(high, g + 1)
                    dve.tensor_tensor(flat, flat, part[0], ALU.subtract).then_inc(rest, 1)
                for k in range(2):
                    g = b * 2 + k
                    flat = qk[k][:, :, :, :].rearrange("p o c s -> p (o c s)")
                    part = [parts[k][:, i, :, :, :].rearrange("p o c s -> p (o c s)") for i in range(3)]
                    dve.wait_ge(mid, g + 1)
                    dve.tensor_tensor(part[2], flat, part[1], ALU.subtract).then_inc(low, 1)

            over_rounds(dve, one)

        @block.gpsimd
        def _(pool):
            def one(b):
                for k in range(2):
                    inverse_root(pool, keep, variance[k][:, :], scale[k][:, :], ln1, b * 2 + k)
                for k in range(2):
                    g = b * 2 + k
                    inverse_root(pool, keep, variance[k][:, :], scale[k][:, :], ln2, g)
                    pool.wait_ge(x1_ready, g + 1)
                    reused(pool, x1_out[k], b * 16)
                    pool.tensor_tensor(x1_bo[k][:, :, :], x1[k][:, :, :], broadcast_groups(keep["bo"][:, :]), ALU.add)\
                        .then_inc(x1_bo_ready, 1)
                for k in range(2):
                    g = b * 2 + k
                    pool.wait_ge(qk_copied, g + 1)
                    reused(pool, parts_out[k], b * 16 * 9)
                    pool.tensor_copy(parts[k][:, 0, :, :, :].rearrange("p o c s -> p (o c s)"),
                                     qk[k][:, :, :, :].rearrange("p o c s -> p (o c s)")).then_inc(high, 1)
                for k in range(2):
                    g = b * 2 + k
                    at_once(pool, rest, g + 1)
                    pool.tensor_copy(parts[k][:, 1, :, :, :].rearrange("p o c s -> p (o c s)"),
                                     qk[k][:, :, :, :].rearrange("p o c s -> p (o c s)")).then_inc(mid, 1)

            over_rounds(pool, one)


def attention_phase(nc, keep, a):
    with ExitStack() as ctx:
        def sb(name, shape, dt=F32):
            return ctx.enter_context(nc.sbuf_tensor("at_" + name, shape, dt))

        def psum(name, shape):
            return ctx.enter_context(nc.psum_tensor("at_" + name, shape, F32))

        def sem(name):
            return ctx.enter_context(nc.semaphore("at_" + name))

        def sems(name, n):
            return [sem(f"{name}{k}") for k in range(n)]

        pos_keys = sb("pos_keys", [K6, H, S], BF16)
        pos_out = sb("pos_out", [P, RING, S])
        pos_in = sb("pos_in", [P, RING, S])
        score = sb("score", [P, RING, S])
        row_max = sb("row_max", [P, RING])
        neg_max = sb("neg_max", [P, RING])
        prob = [sb(f"prob{k}", [P, TILES, QUAD * P]) for k in range(2)]
        q_u, q_v, keys = ([sb(f"{n}{k}", [K6, S], BF16) for k in range(2)] for n in ("q_u", "q_v", "keys"))
        v_in = [sb(f"v_in{k}", [P, P]) for k in range(2)]
        v_aug = [sb(f"v_aug{k}", [P, TILES, VW]) for k in range(2)]
        head_T = sb("head_T", [P, QUAD * P])
        inverse = sb("inverse", [P, QUAD])
        head = [sb(f"head{k}", [P, TILES * DH]) for k in range(2)]
        ps_pos, ps_con, ps_turn = (psum(n, [P, 2, 512]) for n in ("ps_pos", "ps_con", "ps_turn"))
        ps_pv, ps_head = psum("ps_pv", [P, 512]), psum("ps_head", [P, QUAD, P])

        packed = sem("packed")
        written, read = sems("written", RING), sems("read", RING)
        qv_in, qk_in, vals_in, head_out = (sems(n, 2) for n in ("qv_in", "qk_in", "vals_in", "head_out"))
        (pos_mm, pos_copied, con_mm, scored, negated, shifted, turned, exped, pv_mm, pv_copied, head_mm, inverted,
         normed, v_ready, cleared) = (
            sem(n) for n in ("pos_mm", "pos_copied", "con_mm", "scored", "negated", "shifted", "turned", "exped",
                             "pv_mm", "pv_copied", "head_mm", "inverted", "normed", "v_ready", "cleared"))

        class Tile:

            def __init__(self, r, t):
                self.r, self.t = r, t
                self.unit_in_body, self.i = t // TILES, t % TILES
                self.slot, self.side = t % RING, self.unit_in_body % 2

            def count(self, each=1, add=0):
                return self.r * (BODY * each) + (self.t * each + add)

            def rounds(self, n, add=0):
                return self.r * (16 * BODY // n) + 16 * (self.t // n + add)

            def units(self, each=1, add=0):
                return self.r * (2 * each) + (self.unit_in_body * each + add)

            def quads(self, add=0):
                return self.r * (BODY // QUAD) + (self.t // QUAD + add)

            def real(self):
                return not isinstance(self.r, int) or 0 <= self.r * BODY + self.t < NT

            def past(self, n):
                return not isinstance(self.r, int) or self.r * BODY + self.t - n >= 0

            def head_batch(self):
                r = self.r + self.unit_in_body // 2
                return r // (B // 2), (r % (B // 2)) * 2 + self.side

        def rounds(eng, step):
            last = NT // BODY - 1
            for t in range(BODY):
                step(0, t)
            with eng.Fori(1, last) as r:
                for t in range(BODY):
                    step(r, t)
            for t in range(BODY + 8):
                step(last, t)

        score_dram = a["scores"]
        block = ctx.enter_context(nc.Block())

        @block.sync
        def _(sp):
            def part_rows(dst, operand, order, u, sem_):
                h, b = u.head_batch()
                src = a["qk_parts"][operand, :, b, :, :]
                if order is LEFT_PARTS:
                    runs = [(0, 0, 3, True), (3, 1, 2, True), (5, 2, 1, True)]
                else:
                    runs = [(0, 0, 3, False), (3, 0, 2, False), (5, 0, 1, False)]
                for g, part, n, repeat in runs:
                    if repeat:
                        rows = src[part, bass.ds(h * DH, DH), :]
                        rows = rows.unsqueeze(0).to_broadcast([n, DH, S])
                    else:
                        rows = src[part:part + n, bass.ds(h * DH, DH), :]
                    sp.dma_start(dst[DH * g:DH * (g + n), :], rows).then_inc(sem_, 16)

            def load_qv(u):
                if u.past(BODY):
                    at_once(sp, pos_mm, u.units(TILES, -TILES))
                part_rows(q_v[u.side], 1, LEFT_PARTS, u, qv_in[u.side])

            def load_qk(u):
                if u.past(BODY):
                    at_once(sp, con_mm, u.units(TILES, -TILES))
                    at_once(sp, v_ready, u.units(1, -1))
                part_rows(q_u[u.side], 0, LEFT_PARTS, u, qk_in[u.side])
                part_rows(keys[u.side], 2, RIGHT_PARTS, u, qk_in[u.side])
                h, b = u.head_batch()
                sp.dma_start(v_in[u.side][:, :], a["values"][h * B + b, :, :]).then_inc(vals_in[u.side], 16)

            def write(w):
                at_once(sp, pos_copied, w.count(1, 1))
                dst = score_dram[w.side, w.i * P * PITCH:(w.i + 1) * P * PITCH]
                sp.dma_start(dst.rearrange("(p c) -> p c", c=PITCH)[:, 1:], pos_out[:, w.slot, :])\
                    .then_inc(written[w.slot], 16)

            def read_back(t):
                at_once(sp, written[t.slot], t.rounds(RING, 1))
                if t.i + 1 < TILES:
                    n = Tile(t.r, t.t + 1)
                    at_once(sp, written[n.slot], n.rounds(RING, 1))
                if t.past(RING):
                    at_once(sp, scored, t.count(1, 1 - RING))
                src = score_dram[t.side, (t.i * P + 1) * S:(t.i * P + 1 + P) * S]
                sp.dma_start(pos_in[:, t.slot, :], src.rearrange("(p c) -> p c", c=S))\
                    .then_inc(read[t.slot], 16)

            def store_head(t):
                at_once(sp, normed, t.units(2, 2))
                h, b = t.head_batch()
                sp.dma_start(a["heads"][h * B + b, :, :], head[t.side][:, :]).then_inc(head_out[t.side], 16)

            def step(r, t):
                w = Tile(r, t + LEAD)
                if w.real():
                    if w.i == 0 and Tile(r, t + LEAD + TILES).real():
                        load_qv(Tile(r, t + LEAD + TILES))
                    write(w)
                back = Tile(r, t + LEAD - READ_LAG)
                if back.real():
                    read_back(back)
                if t % TILES == 1 and Tile(r, t - 1 + TILES).real():
                    load_qk(Tile(r, t - 1 + TILES))
                done = Tile(r, t - TILES)
                if t % TILES == 3 and done.real():
                    store_head(done)

            for g, k in enumerate(RIGHT_PARTS):
                sp.dma_start(pos_keys[DH * g:DH * (g + 1), :, :],
                             a["pos_parts"][k].rearrange("(h d) m -> d h m", d=DH)).then_inc(packed, 16)
            load_qv(Tile(0, 0))
            load_qv(Tile(0, TILES))
            load_qk(Tile(0, 0))
            for w in range(LEAD):
                write(Tile(0, w))
                if w >= READ_LAG:
                    read_back(Tile(0, w - READ_LAG))
            rounds(sp, step)
            for k in range(2):
                sp.wait_ge(head_out[k], 16 * UNITS // 2)

        @block.tensor
        def _(pe):
            def positional(t):
                pos_head, _ = t.head_batch()
                if t.i == 0:
                    pe.wait_ge(qv_in[t.side], t.r * 48 + (t.unit_in_body // 2 + 1) * 48)
                if t.past(1):
                    pe.wait_ge(pos_copied, t.count())
                for n in range(2):
                    ins = pe.matmul(ps_pos[:, n, :], q_v[t.side][:, t.i * P:(t.i + 1) * P],
                                    pos_keys[:, bass.ds(pos_head, 1), n * 512:(n + 1) * 512]
                                    .rearrange("p a m -> p (a m)"), start=True, stop=True)
                ins.then_inc(pos_mm, 1)

            def content(t):
                if t.i == 0:
                    pe.wait_ge(qk_in[t.side], t.r * 96 + (t.unit_in_body // 2 + 1) * 96)
                if t.past(1):
                    pe.wait_ge(scored, t.count())
                for n in range(2):
                    ins = pe.matmul(ps_con[:, n, :], q_u[t.side][:, t.i * P:(t.i + 1) * P],
                                    keys[t.side][:, n * 512:(n + 1) * 512], start=True, stop=True)
                ins.then_inc(con_mm, 1)

            def turn(t):
                pe.wait_ge(shifted, t.count(1, 1))
                for n in range(2):
                    if t.past(1):
                        pe.wait_ge(exped, t.count(2, n - 1))
                    for j in range(4):
                        kt = 4 * n + j
                        ins = pe.transpose(ps_turn[:, n, j * P:(j + 1) * P],
                                           score[:, t.slot, kt * P:(kt + 1) * P], keep["ident"][:, :])
                    ins.then_inc(turned, 1)

            def times_values(t):
                pe.wait_ge(v_ready, t.units(1, 1))
                pe.wait_ge(exped, t.count(2, 2 * QUAD))
                if t.past(QUAD):
                    pe.wait_ge(pv_copied, t.quads())
                for kt in range(TILES):
                    g = kt % 4
                    ins = pe.matmul(ps_pv[VW * g:VW * (g + 1), :], v_aug[t.side][:, kt, :],
                                    prob[t.t // QUAD % 2][:, kt, :], start=(kt < 4), stop=(kt >= 4))
                ins.then_inc(pv_mm, 1)

            def fold(t):
                pe.wait_ge(pv_copied, t.quads(1))
                if t.past(QUAD):
                    pe.wait_ge(normed, t.quads())
                for k in range(QUAD):
                    ins = pe.matmul(ps_head[:, k, 0:VW], head_T[:, k * P:(k + 1) * P], keep["fold"][:, :],
                                    start=True, stop=True)
                ins.then_inc(head_mm, 1)

            def step(r, t):
                if t % QUAD == 3 and Tile(r, t - 7).real():
                    fold(Tile(r, t - 7))
                if Tile(r, t + LEAD).real():
                    positional(Tile(r, t + LEAD))
                if Tile(r, t).real():
                    content(Tile(r, t))
                if t % QUAD == 1 and Tile(r, t - 5).real():
                    times_values(Tile(r, t - 5))
                if Tile(r, t - 1).real():
                    turn(Tile(r, t - 1))

            pe.wait_ge(packed, 16 * len(RIGHT_PARTS))
            pe.wait_ge(cleared, 1)
            for t in range(LEAD):
                positional(Tile(0, t))
            rounds(pe, step)

        @block.scalar
        def _(act):
            def copy_positional(t):
                act.wait_ge(pos_mm, t.count(1, 1))
                if t.past(RING):
                    act.wait_ge(written[t.slot], t.rounds(RING))
                act.activation(pos_out[:, t.slot, :], ps_pos[:, :, :].rearrange("p a m -> p (a m)"), ACT.Copy)\
                    .then_inc(pos_copied, 1)

            def exponentials(t):
                if t.i % QUAD == 0 and t.past(2 * QUAD):
                    act.wait_ge(pv_mm, t.quads(-1))
                for n in range(2):
                    act.wait_ge(turned, t.count(2, n + 1))
                    k = t.t % QUAD
                    act.activation(prob[t.t // QUAD % 2][:, 4 * n:4 * n + 4, k * P:(k + 1) * P],
                                   ps_turn[:, n, :].rearrange("p (j i) -> p j i", i=P), ACT.Exp)\
                        .then_inc(exped, 1)

            def step(r, t):
                if Tile(r, t + LEAD).real():
                    copy_positional(Tile(r, t + LEAD))
                if Tile(r, t - 1).real():
                    exponentials(Tile(r, t - 1))

            for t in range(LEAD):
                copy_positional(Tile(0, t))
            rounds(act, step)

        @block.vector
        def _(dve):
            def total(t):
                dve.wait_ge(con_mm, t.count(1, 1))
                dve.wait_ge(read[t.slot], t.rounds(RING, 1))
                if t.past(RING):
                    dve.wait_ge(turned, t.count(2, 2 - 2 * RING))
                dve.nop(nofuse=True)
                dve.tensor_tensor_reduce(score[:, t.slot, :], ps_con[:, :, :].rearrange("p a m -> p (a m)"),
                                         pos_in[:, t.slot, :], SCALE, -3.0e38, ALU.add, ALU.max,
                                         row_max[:, t.slot:t.slot + 1]).then_inc(scored, 1)
                dve.wait_ge(scored, t.count(1, 1))
                dve.tensor_scalar(neg_max[:, t.slot:t.slot + 1], row_max[:, t.slot:t.slot + 1], -1.0, None,
                                  ALU.mult).then_inc(negated, 1)

            def copy_products(t):
                dve.wait_ge(pv_mm, t.quads(1))
                if t.past(QUAD):
                    dve.wait_ge(head_mm, t.quads())
                dve.tensor_copy(head_T[:, :], ps_pv[:, :]).then_inc(pv_copied, 1)

            def normalise(t):
                dve.wait_ge(head_mm, t.quads(1))
                if t.past(QUAD):
                    dve.wait_ge(normed, t.quads())
                dve.reciprocal(inverse[:, :], ps_head[:, :, DH]).then_inc(inverted, 1)
                dve.wait_ge(inverted, t.quads(1))
                if t.i == 0 and t.past(BODY):
                    dve.wait_ge(head_out[t.side], t.r * 16 + 16 * (t.unit_in_body // 2))
                q = t.i // QUAD
                dve.tensor_tensor(head[t.side][:, :].rearrange("p (t d) -> p t d", d=DH)[:, QUAD * q:QUAD * (q + 1), :],
                                  ps_head[:, :, 0:DH], inverse[:, :].unsqueeze(2).to_broadcast([P, QUAD, DH]),
                                  ALU.mult).then_inc(normed, 1)

            def step(r, t):
                if Tile(r, t).real():
                    total(Tile(r, t))
                if t % QUAD == 2 and Tile(r, t - 6).real():
                    copy_products(Tile(r, t - 6))
                if t % QUAD == 3 and Tile(r, t - 7).real():
                    normalise(Tile(r, t - 7))

            rounds(dve, step)

        @block.gpsimd
        def _(pool):
            def less_maximum(t):
                at_once(pool, negated, t.count(1, 1))
                pool.tensor_scalar(score[:, t.slot, :], score[:, t.slot, :], neg_max[:, t.slot:t.slot + 1], 1.0,
                                   ALU.add, ALU.mult).then_inc(shifted, 1)

            def copy_values(t):
                pool.wait_ge(vals_in[t.side], t.r * 16 + 16 * (t.unit_in_body // 2 + 1))
                if t.past(BODY):
                    pool.wait_ge(pv_mm, t.units(2, -2))
                pool.nop(nofuse=True)
                pool.tensor_copy(v_aug[t.side][:, :, 0:DH], v_in[t.side][:, :].rearrange("p (j d) -> p j d", d=DH))\
                    .then_inc(v_ready, 1)

            def step(r, t):
                if Tile(r, t).real():
                    less_maximum(Tile(r, t))
                    if t % TILES == 0:
                        copy_values(Tile(r, t))

            for k in range(2):
                pool.memset(v_aug[k][:, :, DH:DH + 1], 1.0)
                ins = pool.memset(v_aug[k][:, :, DH + 1:VW], 0.0)
            ins.then_inc(cleared, 1)
            rounds(pool, step)


def closing_phase(nc, keep, a):
    with ExitStack() as ctx:
        def pair(name, shape, dt=F32):
            return [ctx.enter_context(nc.sbuf_tensor(f"cl_{name}{k}", shape, dt)) for k in range(2)]

        def sem(name):
            return ctx.enter_context(nc.semaphore("cl_" + name))

        heads = pair("heads", [P, H, GROUP * DH])
        x1_bo, x2, z, act_in, out, by_row = (
            pair(n, [P, GROUP, D]) for n in ("x1_bo", "x2", "z", "act_in", "out", "by_row"))
        head_T, zT = pair("head_T", [P, C, ROWS]), pair("zT", [P, C, ROWS])
        stats, moments = pair("stats", [P, GROUP, 6]), pair("moments", [P, GROUP, 2])
        scale, variance = pair("scale", [P, GROUP]), pair("variance", [P, GROUP])
        ps = [ctx.enter_context(nc.psum_tensor(f"cl_ps{k}", [P, 4, 512], F32)) for k in range(2)]
        rows_in, out_done = ([sem(f"{n}{k}") for k in range(2)] for n in ("rows_in", "out_done"))
        ln = [sem("ln_" + n) for n in ("stats", "moments", "variance", "scale", "out")]
        regrouped, turned1, headT, proj, x2_ready, turned2, zT_ready, ffn, biased, tanhed, out_ready = (
            sem(n) for n in ("regrouped", "turned1", "headT", "proj", "x2_ready", "turned2", "zT_ready", "ffn", "biased",
                             "tanhed", "out_ready"))
        x1_rows = a["x1"].rearrange("(g t p) d -> p g t d", p=P, t=GROUP)
        out_rows = a["out"].rearrange("b (g t p) d -> p (b g) t d", p=P, t=GROUP)
        head_rows = a["heads"].rearrange("(h b) p n -> b p h n", b=B)
        block = ctx.enter_context(nc.Block())

        @block.sync
        def _(sp):
            def load(b, k):
                w = GROUP * DH
                sp.dma_start(heads[k][:, :, :], head_rows[b, :, :, k * w:(k + 1) * w]).then_inc(rows_in[k], 16)
                sp.dma_start(x1_bo[k][:, :, :], x1_rows[:, b * 2 + k, :, :]).then_inc(rows_in[k], 16)

            for k in range(2):
                load(0, k)
            def one(b):
                for k in range(2):
                    sp.wait_ge(x2_ready, b * 2 + (k + 1))
                    load((b + 1) % B, k)
                for k in range(2):
                    sp.wait_ge(out_ready, b * 2 + (k + 1))
                    sp.dma_start(out_rows[:, b * 2 + k, :, :], out[k][:, :, :]).then_inc(out_done[k], 16)

            over_rounds(sp, one)
            for k in range(2):
                sp.wait_ge(rows_in[k], 32 * (B + 1))
                sp.wait_ge(out_done[k], 16 * B)

        @block.tensor
        def _(pe):
            def one(b):
                for k in range(2):
                    pe.wait_ge(regrouped, b * 2 + (k + 1))
                    turn_rows(pe, ps[k], lambda t, c: by_row[k][:, t, c * P:(c + 1) * P], keep["ident"])\
                        .then_inc(turned1, 1)
                for k in range(2):
                    g = b * 2 + k
                    pe.wait_ge(headT, g + 1)
                    reused(pe, biased, b * 2)
                    rows_times(pe, ps[k][:, 2:4, :], head_T[k], keep["wo"]).then_inc(proj, 1)
                for k in range(2):
                    pe.wait_ge(ln[4], b * 2 + (k + 1))
                    turn_rows(pe, ps[k], lambda t, c: z[k][:, t, c * P:(c + 1) * P], keep["ident"])\
                        .then_inc(turned2, 1)
                for k in range(2):
                    pe.wait_ge(zT_ready, b * 2 + (k + 1))
                    rows_times(pe, ps[k][:, 2:4, :], zT[k], keep["w3"]).then_inc(ffn, 1)

            over_rounds(pe, one)

        @block.scalar
        def _(act):
            def one(b):
                for k in range(2):
                    act.wait_ge(turned1, b * 2 + (k + 1))
                    act.activation(head_T[k][:, :, :], ps[k][:, 0:2, :], ACT.Copy).then_inc(headT, 1)
                for k in range(2):
                    act.wait_ge(turned2, b * 2 + (k + 1))
                    act.activation(zT[k][:, :, :], ps[k][:, 0:2, :], ACT.Copy).then_inc(zT_ready, 1)
                for k in range(2):
                    act.wait_ge(biased, b * 2 + (k + 1))
                    act.activation(act_in[k][:, :, :], act_in[k][:, :, :], ACT.Tanh).then_inc(tanhed, 1)

            over_rounds(act, one)

        @block.vector
        def _(dve):
            def one(b):
                for k in range(2):
                    g = b * 2 + k
                    dve.wait_ge(proj, g + 1)
                    dve.wait_ge(rows_in[k], b * 32 + 32)
                    reused(dve, out_ready, b * 2)
                    dve.tensor_tensor(x2[k][:, :, :], ps[k][:, 2:4, :].rearrange("p a (t d) -> p (a t) d", d=D),
                                      x1_bo[k][:, :, :], ALU.add).then_inc(x2_ready, 1)
                    dve.wait_ge(x2_ready, g + 1)
                    layer_norm(dve, x2[k], stats[k], moments[k], variance[k][:, :], scale[k][:, :], ln, g, z[k], False)
                for k in range(2):
                    g = b * 2 + k
                    dve.wait_ge(ffn, g + 1)
                    dve.tensor_tensor(act_in[k][:, :, :], ps[k][:, 2:4, :].rearrange("p a (t d) -> p (a t) d", d=D),
                                      broadcast_groups(keep["b_ffn"][:, :]), ALU.add).then_inc(biased, 1)
                for k in range(2):
                    g = b * 2 + k
                    dve.wait_ge(tanhed, g + 1)
                    reused(dve, out_done[k], b * 16)
                    dve.scalar_tensor_tensor(out[k][:, :, :].rearrange("p t d -> p (t d)"),
                                             act_in[k][:, :, :].rearrange("p t d -> p (t d)"), 0.5,
                                             x2[k][:, :, :].rearrange("p t d -> p (t d)"), ALU.mult, ALU.add)\
                        .then_inc(out_ready, 1)

            over_rounds(dve, one)


        @block.gpsimd
        def _(pool):
            def one(b):
                for k in range(2):
                    pool.wait_ge(rows_in[k], b * 32 + 32)
                    reused(pool, turned1, b * 2)
                    pool.tensor_copy(by_row[k][:, :, :].rearrange("p t (h d) -> p t h d", d=DH),
                                     heads[k][:, :, :].rearrange("p h (t d) -> p t h d", d=DH))\
                        .then_inc(regrouped, 1)
                for k in range(2):
                    inverse_root(pool, keep, variance[k][:, :], scale[k][:, :], ln, b * 2 + k)

            over_rounds(pool, one)


def macaron_layer(nc, a):
    def scratch(name, shape, dt=F32):
        a[name] = nc.dram_tensor("scratch_" + name, shape, dt, kind="Internal").ap()

    scratch("scores", [2, S * PITCH])
    scratch("pos_parts", [3, D, S], BF16)
    scratch("qk_parts", [3, 3, B, D, S], BF16)
    scratch("values", [UNITS, P, P])
    scratch("heads", [UNITS, P, P])
    scratch("x1", [B * S, D])
    with ExitStack() as ctx:
        def sb(name, shape, dt=F32):
            return ctx.enter_context(nc.sbuf_tensor("keep_" + name, shape, dt))

        keep = {n: sb(n, [P, C, D]) for n in ("wq", "wk", "wv", "wo", "w3")}
        keep |= {n: sb(n, [P, D]) for n in ("b_ffn", "bo", "bv")}
        keep["b_qk"] = sb("b_qk", [P, 3, C])
        keep["minus_half"] = sb("minus_half", [P, GROUP])
        keep["ident"] = sb("ident", [P, P])
        keep["fold"] = sb("fold", [P, VW])
        setup_phase(nc, keep, a)
        dense_phase(nc, keep, a)
        attention_phase(nc, keep, a)
        closing_phase(nc, keep, a)


_INS = ['L0_attn_x', 'L0_attn_ln_g', 'L0_attn_ln_b', 'L0_attn_Wq', 'L0_attn_bq', 'L0_attn_Wk', 'L0_attn_bk',
        'L0_attn_Wv', 'L0_attn_bv', 'L0_attn_Wp', 'L0_attn_Wo', 'L0_attn_bo', 'L0_attn_u_bias', 'L0_attn_v_bias',
        'L0_ffn_weight', 'L0_ffn_aux_weight1', 'L0_ffn_aux_weight2', 'L0_ffn_bias']


def constants():
    import math
    import numpy as np
    pos = np.arange(S, dtype=np.float32)[:, None]
    div = np.exp(np.arange(0, D, 2, dtype=np.float32) * np.float32(-math.log(10000.0) / D))
    ang = pos * div
    pe = np.stack([np.sin(ang), np.cos(ang)], axis=-1).reshape(S, D)
    return {"pe_T": np.ascontiguousarray(pe.T, dtype=np.float32), "ident": np.eye(P, dtype=np.float32),
            "fold": np.tile(np.eye(VW, dtype=np.float32), (P // VW, 1))}


def kernel(**inputs):
    import numpy as _np
    import concourse.bacc as _bacc
    from concourse import mybir as _mybir
    from concourse.bass_utils import run_bass_kernel_spmd as _run

    nc = _bacc.Bacc("TRN2", target_bir_lowering=False, num_devices=1)
    arrays, args = {}, {}
    given = {n: _np.ascontiguousarray(inputs[n]) for n in _INS} | constants()
    for name, x in given.items():
        arrays[f"in_{name}_dram"] = x
        args[name] = nc.dram_tensor(f"in_{name}_dram", x.shape, _mybir.dt.from_np(x.dtype), kind="ExternalInput").ap()
    args["out"] = nc.dram_tensor("out_0_dram", [B, S, D], F32, kind="ExternalOutput").ap()
    macaron_layer(nc, args)
    r = _run(nc, [arrays], core_ids=[0])
    return r.results[0]["out_0_dram"]
```

```python
from contextlib import ExitStack

import concourse.bass as bass
from concourse import mybir

F32 = mybir.dt.float32
BF16 = mybir.dt.bfloat16
ALU = mybir.AluOpType
ACT = mybir.ActivationFunctionType

P = 128
B, S, D, H = 8, 1024, 256, 16
DH = D // H
C = D // P
EPS = 1e-5
SCALE = DH ** -0.5

LEFT_PARTS = [0, 0, 0, 1, 1, 2]
RIGHT_PARTS = [0, 1, 2, 0, 1, 0]
K6 = DH * len(LEFT_PARTS)

TILES = S // P
UNITS = H * B
NT = UNITS * TILES
BODY = 2 * TILES
LEAD = 6
READ_LAG = 3
RING = 8
PITCH = S + 1
QUAD = 4
VW = 32

GROUP = 4
ROWS = GROUP * P
GROUPS = B * S // ROWS


def at_once(eng, sem, value):
    eng.wait_ge(sem, value)
    eng.nop(nofuse=True)


def reused(eng, sem, value):
    if not isinstance(value, int) or value > 0:
        eng.wait_ge(sem, value)
        eng.nop(nofuse=True)


def over_rounds(eng, step):
    step(0, None)
    step(1, 0)
    with eng.Fori(2, B) as b:
        step(b, b - 1)
    step(None, B - 1)


def broadcast_groups(row, n=GROUP):
    return row.unsqueeze(1).to_broadcast([P, n, D])


def layer_norm(eng, src, stats, moments, variance, scale, sems, at, out, twice):
    s_stats, s_moments, s_variance, s_scale, s_out = sems
    for t in range(GROUP):
        ins = eng.bn_stats(stats[:, t, :], src[:, t, :])
    ins.then_inc(s_stats, 1)
    at_once(eng, s_stats, at + 1)
    for t in range(GROUP):
        ins = eng.bn_aggr(moments[:, t, :], stats[:, t, :])
    ins.then_inc(s_moments, 1)
    eng.wait_ge(s_moments, at + 1)
    if twice:
        ins = eng.tensor_scalar(variance, moments[:, :, 1], 1.0 + EPS, EPS * EPS, ALU.mult, ALU.add)
    else:
        ins = eng.tensor_scalar(variance, moments[:, :, 1], EPS, None, ALU.add)
    ins.then_inc(s_variance, 1)
    eng.wait_ge(s_scale, at + 1)
    for t in range(GROUP):
        ins = eng.tensor_scalar(out[:, t, :], src[:, t, :], moments[:, t, 0:1], scale[:, t:t + 1],
                                ALU.subtract, ALU.mult)
    ins.then_inc(s_out, 1)


def inverse_root(pool, keep, variance, scale, sems, at):
    pool.wait_ge(sems[2], at + 1)
    pool.tensor_tensor(scale, variance, keep["minus_half"][:, :], ALU.pow).then_inc(sems[3], 1)


def turn_rows(eng, bank0, src, ident):
    for c in range(C):
        for t in range(GROUP):
            ins = eng.transpose(bank0[:, c, t * P:(t + 1) * P], src(t, c), ident[:, :])
    return ins


def rows_times(eng, banks, xT, w):
    for t in range(GROUP):
        for c in range(C):
            ins = eng.matmul(banks[:, t // 2, (t % 2) * D:(t % 2 + 1) * D],
                             xT[:, c, t * P:(t + 1) * P], w[:, c, :], start=(c == 0), stop=(c == C - 1))
    return ins


def setup_phase(nc, keep, a):
    with ExitStack() as ctx:
        def sb(name, shape, dt=F32):
            return ctx.enter_context(nc.sbuf_tensor("su_" + name, shape, dt))

        def sem(name):
            return ctx.enter_context(nc.semaphore("su_" + name))

        w_ffn, aux1, aux2, w_pos = (sb(n, [P, C, D]) for n in ("w_ffn", "aux1", "aux2", "w_pos"))
        pe_T = sb("pe_T", [P, C, S])
        turned = sb("turned", [P, 2, C, D])
        aux12 = sb("aux12", [P, C, D])
        ln_b_rep = sb("ln_b_rep", [P, C, P])
        cols = sb("cols", [P, 6, C])
        bv_row = sb("bv_row", [P, D])
        bq_k = sb("bq_k", [P, 2, C])
        pos = sb("pos", [P, C, S])
        parts = sb("parts", [P, 3, C, S], BF16)
        zeros = sb("zeros", [P, 2 * TILES])
        ps = ctx.enter_context(nc.psum_tensor("su_ps", [P, 8, 512], F32))
        loaded, pe_step, act_step, dve_step, stored = (
            sem(n) for n in ("loaded", "pe_step", "act_step", "dve_step", "stored"))
        LN_G, LN_B, BQ, BK, U, V = range(6)

        def chunks(x):
            return x.rearrange("(c p) n -> p c n", p=P)

        def by_feature(x):
            return x.rearrange("(c p) -> p c", p=P)

        loads = [
            (w_ffn[:, :, :], chunks(a["L0_ffn_weight"])), (aux1[:, :, :], chunks(a["L0_ffn_aux_weight1"])),
            (aux2[:, :, :], chunks(a["L0_ffn_aux_weight2"])), (w_pos[:, :, :], chunks(a["L0_attn_Wp"])),
            (keep["wq"][:, :, :], chunks(a["L0_attn_Wq"])), (keep["wk"][:, :, :], chunks(a["L0_attn_Wk"])),
            (keep["wv"][:, :, :], chunks(a["L0_attn_Wv"])), (keep["wo"][:, :, :], chunks(a["L0_attn_Wo"])),
            (pe_T[:, :, :], chunks(a["pe_T"])), (keep["ident"][:, :], a["ident"]), (keep["fold"][:, :], a["fold"]),
            (keep["b_ffn"][:, :], a["L0_ffn_bias"].partition_broadcast(P)),
            (keep["bo"][:, :], a["L0_attn_bo"].partition_broadcast(P)),
            (bv_row[:, :], a["L0_attn_bv"].partition_broadcast(P)),
        ]
        vectors = [(LN_G, a["L0_attn_ln_g"]), (LN_B, a["L0_attn_ln_b"]), (BQ, a["L0_attn_bq"]),
                   (BK, a["L0_attn_bk"]), (U, a["L0_attn_u_bias"].rearrange("h d -> (h d)")),
                   (V, a["L0_attn_v_bias"].rearrange("h d -> (h d)"))]
        n_loads = len(loads) + len(vectors)
        block = ctx.enter_context(nc.Block())

        @block.sync
        def _(sp):
            with nc.allow_non_contiguous_dma(reason="vectors of 256 by feature, and the zero column"):
                for dst, src in loads:
                    sp.dma_start(dst, src).then_inc(loaded, 16)
                for k, v in vectors:
                    sp.dma_start(cols[:, k, :], by_feature(v)).then_inc(loaded, 16)
                sp.wait_ge(dve_step, 1)
                sp.dma_start(a["scores"].rearrange("n (t p c) -> p (n t) c", p=P, c=PITCH)[:, :, 0], zeros[:, :])\
                    .then_inc(stored, 16)
            for k, need in enumerate((7, 9, 10)):
                sp.wait_ge(dve_step, need)
                sp.dma_start(a["pos_parts"][k].rearrange("(c p) m -> p c m", p=P), parts[:, k, :, :])\
                    .then_inc(stored, 16)
            sp.wait_ge(stored, 64)

        @block.tensor
        def _(pe):
            pe.wait_ge(loaded, 16 * n_loads)
            for k, w in enumerate((w_ffn, aux1)):
                for c in range(C):
                    for r in range(C):
                        ins = pe.transpose(ps[:, 2 * k + c, r * P:(r + 1) * P], w[:, r, c * P:(c + 1) * P],
                                           keep["ident"][:, :])
            ins.then_inc(pe_step, 1)
            for c in range(C):
                for n in range(2):
                    for k in range(C):
                        ins = pe.matmul(ps[:, 4 + 2 * c + n, :], w_pos[:, k, c * P:(c + 1) * P],
                                        pe_T[:, k, n * 512:(n + 1) * 512], start=(k == 0), stop=(k == C - 1))
            ins.then_inc(pe_step, 1)
            pe.wait_ge(act_step, 1)
            for r in range(C):
                for k in range(C):
                    ins = pe.matmul(ps[:, 0, r * D:(r + 1) * D], turned[:, 1, k, r * P:(r + 1) * P],
                                    aux2[:, k, :], start=(k == 0), stop=(k == C - 1))
            ins.then_inc(pe_step, 1)
            pe.wait_ge(dve_step, 2)
            for k in range(C):
                pe.matmul(ps[:, 1, 0:D], ln_b_rep[:, k, :], keep["wv"][:, k, :], start=(k == 0), stop=(k == C - 1))
            for i, w in enumerate(("wq", "wk")):
                for c in range(C):
                    for k in range(C):
                        ins = pe.matmul(ps[:, 2, 2 * i + c:2 * i + c + 1], keep[w][:, k, c * P:(c + 1) * P],
                                        cols[:, LN_B, k:k + 1], start=(k == 0), stop=(k == C - 1))
            ins.then_inc(pe_step, 1)
            pe.wait_ge(act_step, 2)
            for r in range(C):
                for k in range(C):
                    ins = pe.matmul(ps[:, 3, r * D:(r + 1) * D], turned[:, 0, k, r * P:(r + 1) * P],
                                    aux12[:, k, :], start=(k == 0), stop=(k == C - 1))
            ins.then_inc(pe_step, 1)

        @block.scalar
        def _(act):
            act.wait_ge(pe_step, 1)
            act.activation(turned[:, :, :, :].rearrange("p k c n -> p (k c) n"), ps[:, 0:4, 0:D], ACT.Copy)\
                .then_inc(act_step, 1)
            act.wait_ge(pe_step, 3)
            act.activation(aux12[:, :, :].rearrange("p c n -> p (c n)"), ps[:, 0, :], ACT.Copy).then_inc(act_step, 1)
            act.wait_ge(pe_step, 5)
            act.activation(keep["w3"][:, :, :].rearrange("p c n -> p (c n)"), ps[:, 3, :], ACT.Copy)\
                .then_inc(act_step, 1)

        @block.vector
        def _(dve):
            dve.memset(keep["minus_half"][:, :], -0.5)
            dve.memset(zeros[:, :], 0.0).then_inc(dve_step, 1)
            dve.wait_ge(loaded, 16 * n_loads)
            for c in range(C):
                ins = dve.tensor_copy(ln_b_rep[:, c, :], cols[:, LN_B, c:c + 1].to_broadcast([P, P]))
            ins.then_inc(dve_step, 1)
            dve.wait_ge(pe_step, 4)
            dve.tensor_tensor(keep["bv"][:, :], ps[:, 1, 0:D], bv_row[:, :], ALU.add)
            dve.tensor_tensor(bq_k[:, :, :].rearrange("p i c -> p (i c)"), ps[:, 2, 0:4],
                              cols[:, BQ:BK + 1, :].rearrange("p i c -> p (i c)"), ALU.add).then_inc(dve_step, 1)
            dve.wait_ge(dve_step, 3)
            dve.tensor_tensor(keep["b_qk"][:, 0, :], bq_k[:, 0, :], cols[:, U, :], ALU.add)
            dve.tensor_tensor(keep["b_qk"][:, 1, :], bq_k[:, 0, :], cols[:, V, :], ALU.add)
            dve.tensor_copy(keep["b_qk"][:, 2, :], bq_k[:, 1, :]).then_inc(dve_step, 1)
            for w in ("wq", "wk", "wv"):
                for c in range(C):
                    ins = dve.tensor_scalar(keep[w][:, c, :], keep[w][:, c, :], cols[:, LN_G, c:c + 1], None, ALU.mult)
            ins.then_inc(dve_step, 1)
            dve.wait_ge(pe_step, 2)
            dve.tensor_copy(pos[:, :, :].rearrange("p c m -> p (c m)"),
                            ps[:, 4:8, :].rearrange("p b m -> p (b m)")).then_inc(dve_step, 1)
            dve.wait_ge(dve_step, 6)
            dve.tensor_copy(parts[:, 0, :, :], pos[:, :, :]).then_inc(dve_step, 1)
            dve.wait_ge(dve_step, 7)
            dve.tensor_tensor(pos[:, :, :], pos[:, :, :], parts[:, 0, :, :], ALU.subtract).then_inc(dve_step, 1)
            dve.wait_ge(dve_step, 8)
            dve.tensor_copy(parts[:, 1, :, :], pos[:, :, :]).then_inc(dve_step, 1)
            dve.wait_ge(dve_step, 9)
            dve.tensor_tensor(parts[:, 2, :, :], pos[:, :, :], parts[:, 1, :, :], ALU.subtract).then_inc(dve_step, 1)


def dense_phase(nc, keep, a):
    with ExitStack() as ctx:
        def pair(name, shape, dt=F32):
            return [ctx.enter_context(nc.sbuf_tensor(f"de_{name}{k}", shape, dt)) for k in range(2)]

        def sem(name):
            return ctx.enter_context(nc.semaphore("de_" + name))

        x, x1, x1_bo, z1, z2, act_in = (
            pair(n, [P, GROUP, D]) for n in ("x", "x1", "x1_bo", "z1", "z2", "act_in"))
        z1T, z2T = pair("z1T", [P, C, ROWS]), pair("z2T", [P, C, ROWS])
        (stats1, moments1, variance1, scale1), (stats2, moments2, variance2, scale2) = (
            (pair(f"stats{n}_", [P, GROUP, 6]), pair(f"moments{n}_", [P, GROUP, 2]),
             pair(f"variance{n}_", [P, GROUP]), pair(f"scale{n}_", [P, GROUP])) for n in (1, 2))
        qk = pair("qk", [P, 3, C, ROWS])
        parts = pair("parts", [P, 3, 3, C, ROWS], BF16)
        values = ctx.enter_context(nc.sbuf_tensor("de_values", [P, UNITS * P], F32))
        ps = [ctx.enter_context(nc.psum_tensor(f"de_ps{k}", [P, 4, 512], F32)) for k in range(2)]
        x_in = [sem(f"x_in{k}") for k in range(2)]
        x1_out = [sem(f"x1_out{k}") for k in range(2)]
        parts_out = [sem(f"parts_out{k}") for k in range(2)]
        ln1 = [sem("ln1_" + n) for n in ("stats", "moments", "variance", "scale", "out")]
        ln2 = [sem("ln2_" + n) for n in ("stats", "moments", "variance", "scale", "out")]
        (turned1, zT1, ffn, biased, tanhed, x1_ready, x1_bo_ready, turned2, zT2, qk_mm, q_copied, qk_copied,
         v_mm, v_copied, rest, mid, low, v_out) = (
            sem(n) for n in ("turned1", "zT1", "ffn", "biased", "tanhed", "x1_ready", "x1_bo_ready", "turned2",
                             "zT2", "qk_mm", "q_copied", "qk_copied", "v_mm", "v_copied", "rest", "mid",
                             "low", "v_out"))
        rows = a["L0_attn_x"].rearrange("b (g t p) d -> p (b g) t d", p=P, t=GROUP)
        x1_rows = a["x1"].rearrange("(g t p) d -> p g t d", p=P, t=GROUP)
        qk_dram = a["qk_parts"]
        half = S // ROWS
        block = ctx.enter_context(nc.Block())

        @block.sync
        def _(sp):
            def load(b, k):
                sp.dma_start(x[k][:, :, :], rows[:, b * half + k, :, :]).then_inc(x_in[k], 16)

            def step(b, c):
                if b is not None:
                    for k in range(2):
                        if not isinstance(b, int) or b > 0:
                            sp.wait_ge(x1_ready, b * 2 + (k - 1))
                        load(b, k)
                    for k in range(2):
                        sp.wait_ge(x1_bo_ready, b * 2 + (k + 1))
                        sp.dma_start(x1_rows[:, b * 2 + k, :, :], x1_bo[k][:, :, :]).then_inc(x1_out[k], 16)
                if c is not None:
                    for k in range(2):
                        sp.wait_ge(low, c * 2 + (k + 1))
                        for o in range(3):
                            for part in range(3):
                                dst = qk_dram[o, part, c, :, k * ROWS:(k + 1) * ROWS]
                                sp.dma_start(dst.rearrange("(c p) s -> p c s", p=P), parts[k][:, part, o, :, :])\
                                    .then_inc(parts_out[k], 16)

            over_rounds(sp, step)
            sp.wait_ge(v_copied, GROUPS)
            sp.dma_start(a["values"].rearrange("u p n -> p u n"),
                         values[:, :].rearrange("p (u n) -> p u n", n=P)).then_inc(v_out, 16)
            for k in range(2):
                sp.wait_ge(x1_out[k], 16 * B)
                sp.wait_ge(parts_out[k], 16 * 9 * B)
            sp.wait_ge(v_out, 16)

        @block.tensor
        def _(pe):
            def step(b, c):
                if c is not None:
                    for k in range(2):
                        pe.wait_ge(ln2[4], c * 2 + (k + 1))
                        reused(pe, v_copied, c * 2)
                        turn_rows(pe, ps[k], lambda t, f: z2[k][:, t, f * P:(f + 1) * P], keep["ident"])\
                            .then_inc(turned2, 1)
                if b is not None:
                    for k in range(2):
                        pe.wait_ge(ln1[4], b * 2 + (k + 1))
                        if c is not None:
                            reused(pe, qk_copied, c * 2)
                        turn_rows(pe, ps[k][:, 2:4, :], lambda t, f: z1[k][:, t, f * P:(f + 1) * P], keep["ident"])\
                            .then_inc(turned1, 1)
                    for k in range(2):
                        pe.wait_ge(zT1, b * 2 + (k + 1))
                        rows_times(pe, ps[k][:, 2:4, :], z1T[k], keep["w3"]).then_inc(ffn, 1)
                if c is not None:
                    for k in range(2):
                        pe.wait_ge(zT2, c * 2 + (k + 1))
                        if b is not None:
                            pe.wait_ge(biased, b * 2 + (k + 1))
                        for i, w in enumerate(("wq", "wk")):
                            for f in range(C):
                                for kk in range(C):
                                    ins = pe.matmul(ps[k][:, 2 * i + f, :], keep[w][:, kk, f * P:(f + 1) * P],
                                                    z2T[k][:, kk, :], start=(kk == 0), stop=(kk == C - 1))
                        ins.then_inc(qk_mm, 1)
                    for k in range(2):
                        pe.wait_ge(q_copied, c * 2 + (k + 1))
                        rows_times(pe, ps[k][:, 0:2, :], z2T[k], keep["wv"]).then_inc(v_mm, 1)

            over_rounds(pe, step)

        @block.scalar
        def _(act):
            def step(b, c):
                if c is not None:
                    for k in range(2):
                        act.wait_ge(turned2, c * 2 + (k + 1))
                        reused(act, v_mm, c * 2)
                        act.activation(z2T[k][:, :, :], ps[k][:, 0:2, :], ACT.Copy).then_inc(zT2, 1)
                if b is not None:
                    for k in range(2):
                        act.wait_ge(turned1, b * 2 + (k + 1))
                        reused(act, ffn, b * 2)
                        act.activation(z1T[k][:, :, :], ps[k][:, 2:4, :], ACT.Copy).then_inc(zT1, 1)
                    for k in range(2):
                        act.wait_ge(biased, b * 2 + (k + 1))
                        act.activation(act_in[k][:, :, :], act_in[k][:, :, :], ACT.Tanh).then_inc(tanhed, 1)
                if c is not None:
                    for k in range(2):
                        act.wait_ge(qk_mm, c * 2 + (k + 1))
                        reused(act, low, c * 2)
                        reused(act, parts_out[k], c * 16 * 9)
                        for o in range(3):
                            for f in range(C):
                                for dst in (qk[k][:, o, f, :], parts[k][:, 0, o, f, :]):
                                    ins = act.activation(dst, ps[k][:, 2 * (o // 2) + f, :], ACT.Identity,
                                                         bias=keep["b_qk"][:, o, f:f + 1])
                            if o == 1:
                                ins.then_inc(q_copied, 1)
                        ins.then_inc(qk_copied, 1)
                    for k in range(2):
                        act.wait_ge(rest, c * 2 + (k + 1))
                        act.activation(parts[k][:, 1, :, :, :].rearrange("p o c s -> p (o c s)"),
                                       qk[k][:, :, :, :].rearrange("p o c s -> p (o c s)"), ACT.Copy).then_inc(mid, 1)

            over_rounds(act, step)

        @block.vector
        def _(dve):
            def step(b, c):
                if b is not None:
                    for k in range(2):
                        dve.wait_ge(x_in[k], b * 16 + 16)
                        reused(dve, turned1, b * 2)
                        layer_norm(dve, x[k], stats1[k], moments1[k], variance1[k][:, :], scale1[k][:, :], ln1,
                                   b * 2 + k, z1[k], False)
                    for k in range(2):
                        dve.wait_ge(ffn, b * 2 + (k + 1))
                        dve.tensor_tensor(act_in[k][:, :, :],
                                          ps[k][:, 2:4, :].rearrange("p a (t d) -> p (a t) d", d=D),
                                          broadcast_groups(keep["b_ffn"][:, :]), ALU.add).then_inc(biased, 1)
                    for k in range(2):
                        g = b * 2 + k
                        dve.wait_ge(tanhed, g + 1)
                        reused(dve, x1_bo_ready, b * 2)
                        dve.scalar_tensor_tensor(x1[k][:, :, :].rearrange("p t d -> p (t d)"),
                                                 act_in[k][:, :, :].rearrange("p t d -> p (t d)"), 0.5,
                                                 x[k][:, :, :].rearrange("p t d -> p (t d)"), ALU.mult, ALU.add)\
                            .then_inc(x1_ready, 1)
                        dve.wait_ge(x1_ready, g + 1)
                        reused(dve, turned2, b * 2)
                        layer_norm(dve, x1[k], stats2[k], moments2[k], variance2[k][:, :], scale2[k][:, :], ln2, g,
                                   z2[k], True)
                if c is not None:
                    for k in range(2):
                        flat = qk[k][:, :, :, :].rearrange("p o c s -> p (o c s)")
                        dve.wait_ge(qk_copied, c * 2 + (k + 1))
                        dve.tensor_tensor(flat, flat, parts[k][:, 0, :, :, :].rearrange("p o c s -> p (o c s)"),
                                          ALU.subtract).then_inc(rest, 1)
                    for k in range(2):
                        dve.wait_ge(v_mm, c * 2 + (k + 1))
                        dst = values[:, :].rearrange("p (h bt d) -> p bt h d", h=H, d=DH)
                        dve.tensor_tensor(dst[:, bass.ds(c * TILES + k * GROUP, GROUP), :, :],
                                          ps[k][:, 0:2, :].rearrange("p a (t h d) -> p (a t) h d", h=H, d=DH),
                                          broadcast_groups(keep["bv"][:, :]).rearrange("p t (h d) -> p t h d", d=DH),
                                          ALU.add).then_inc(v_copied, 1)
                    for k in range(2):
                        flat = qk[k][:, :, :, :].rearrange("p o c s -> p (o c s)")
                        part = [parts[k][:, i, :, :, :].rearrange("p o c s -> p (o c s)") for i in range(3)]
                        dve.wait_ge(mid, c * 2 + (k + 1))
                        dve.tensor_tensor(part[2], flat, part[1], ALU.subtract).then_inc(low, 1)

            over_rounds(dve, step)

        @block.gpsimd
        def _(pool):
            def step(b, c):
                if b is not None:
                    for k in range(2):
                        inverse_root(pool, keep, variance1[k][:, :], scale1[k][:, :], ln1, b * 2 + k)
                    for k in range(2):
                        inverse_root(pool, keep, variance2[k][:, :], scale2[k][:, :], ln2, b * 2 + k)
                    for k in range(2):
                        pool.wait_ge(x1_ready, b * 2 + (k + 1))
                        reused(pool, x1_out[k], b * 16)
                        pool.tensor_tensor(x1_bo[k][:, :, :], x1[k][:, :, :], broadcast_groups(keep["bo"][:, :]),
                                           ALU.add).then_inc(x1_bo_ready, 1)

            over_rounds(pool, step)


def attention_phase(nc, keep, a):
    with ExitStack() as ctx:
        def sb(name, shape, dt=F32):
            return ctx.enter_context(nc.sbuf_tensor("at_" + name, shape, dt))

        def psum(name, shape):
            return ctx.enter_context(nc.psum_tensor("at_" + name, shape, F32))

        def sem(name):
            return ctx.enter_context(nc.semaphore("at_" + name))

        def sems(name, n):
            return [sem(f"{name}{k}") for k in range(n)]

        pos_keys = sb("pos_keys", [K6, H, S], BF16)
        pos_out = sb("pos_out", [P, RING, S])
        pos_in = sb("pos_in", [P, RING, S])
        score = sb("score", [P, RING, S])
        row_max = sb("row_max", [P, RING])
        neg_max = sb("neg_max", [P, RING])
        prob = [sb(f"prob{k}", [P, TILES, QUAD * P]) for k in range(2)]
        q_u, q_v, keys = ([sb(f"{n}{k}", [K6, S], BF16) for k in range(2)] for n in ("q_u", "q_v", "keys"))
        v_in = [sb(f"v_in{k}", [P, P]) for k in range(2)]
        v_aug = [sb(f"v_aug{k}", [P, TILES, VW]) for k in range(2)]
        head_T = sb("head_T", [P, QUAD * P])
        inverse = sb("inverse", [P, QUAD])
        head = [sb(f"head{k}", [P, TILES * DH]) for k in range(2)]
        ps_pos, ps_con, ps_turn = (psum(n, [P, 2, 512]) for n in ("ps_pos", "ps_con", "ps_turn"))
        ps_pv, ps_head = psum("ps_pv", [P, 512]), psum("ps_head", [P, QUAD, P])

        packed = sem("packed")
        written, read = sems("written", RING), sems("read", RING)
        qv_in, qk_in, vals_in, head_out = (sems(n, 2) for n in ("qv_in", "qk_in", "vals_in", "head_out"))
        (pos_mm, pos_copied, con_mm, scored, negated, shifted, turned, exped, pv_mm, pv_copied, head_mm, inverted,
         normed, v_ready, cleared) = (
            sem(n) for n in ("pos_mm", "pos_copied", "con_mm", "scored", "negated", "shifted", "turned", "exped",
                             "pv_mm", "pv_copied", "head_mm", "inverted", "normed", "v_ready", "cleared"))

        class Tile:

            def __init__(self, r, t):
                self.r, self.t = r, t
                self.unit_in_body, self.i = t // TILES, t % TILES
                self.slot, self.side = t % RING, self.unit_in_body % 2

            def count(self, each=1, add=0):
                return self.r * (BODY * each) + (self.t * each + add)

            def rounds(self, n, add=0):
                return self.r * (16 * BODY // n) + 16 * (self.t // n + add)

            def units(self, each=1, add=0):
                return self.r * (2 * each) + (self.unit_in_body * each + add)

            def quads(self, add=0):
                return self.r * (BODY // QUAD) + (self.t // QUAD + add)

            def real(self):
                return not isinstance(self.r, int) or 0 <= self.r * BODY + self.t < NT

            def past(self, n):
                return not isinstance(self.r, int) or self.r * BODY + self.t - n >= 0

            def head_batch(self):
                r = self.r + self.unit_in_body // 2
                return r // (B // 2), (r % (B // 2)) * 2 + self.side

        def rounds(eng, step):
            last = NT // BODY - 1
            for t in range(BODY):
                step(0, t)
            with eng.Fori(1, last) as r:
                for t in range(BODY):
                    step(r, t)
            for t in range(BODY + 8):
                step(last, t)

        score_dram = a["scores"]
        block = ctx.enter_context(nc.Block())

        @block.sync
        def _(sp):
            def part_rows(dst, operand, order, u, sem_):
                h, b = u.head_batch()
                src = a["qk_parts"][operand, :, b, :, :]
                if order is LEFT_PARTS:
                    runs = [(0, 0, 3, True), (3, 1, 2, True), (5, 2, 1, True)]
                else:
                    runs = [(0, 0, 3, False), (3, 0, 2, False), (5, 0, 1, False)]
                for g, part, n, repeat in runs:
                    if repeat:
                        rows = src[part, bass.ds(h * DH, DH), :]
                        rows = rows.unsqueeze(0).to_broadcast([n, DH, S])
                    else:
                        rows = src[part:part + n, bass.ds(h * DH, DH), :]
                    sp.dma_start(dst[DH * g:DH * (g + n), :], rows).then_inc(sem_, 16)

            def load_qv(u):
                if u.past(BODY):
                    at_once(sp, pos_mm, u.units(TILES, -TILES))
                part_rows(q_v[u.side], 1, LEFT_PARTS, u, qv_in[u.side])

            def load_qk(u):
                if u.past(BODY):
                    at_once(sp, con_mm, u.units(TILES, -TILES))
                    at_once(sp, v_ready, u.units(1, -1))
                part_rows(q_u[u.side], 0, LEFT_PARTS, u, qk_in[u.side])
                part_rows(keys[u.side], 2, RIGHT_PARTS, u, qk_in[u.side])
                h, b = u.head_batch()
                sp.dma_start(v_in[u.side][:, :], a["values"][h * B + b, :, :]).then_inc(vals_in[u.side], 16)

            def write(w):
                at_once(sp, pos_copied, w.count(1, 1))
                dst = score_dram[w.side, w.i * P * PITCH:(w.i + 1) * P * PITCH]
                sp.dma_start(dst.rearrange("(p c) -> p c", c=PITCH)[:, 1:], pos_out[:, w.slot, :])\
                    .then_inc(written[w.slot], 16)

            def read_back(t):
                at_once(sp, written[t.slot], t.rounds(RING, 1))
                if t.i + 1 < TILES:
                    n = Tile(t.r, t.t + 1)
                    at_once(sp, written[n.slot], n.rounds(RING, 1))
                if t.past(RING):
                    at_once(sp, scored, t.count(1, 1 - RING))
                src = score_dram[t.side, (t.i * P + 1) * S:(t.i * P + 1 + P) * S]
                sp.dma_start(pos_in[:, t.slot, :], src.rearrange("(p c) -> p c", c=S))\
                    .then_inc(read[t.slot], 16)

            def store_head(t):
                at_once(sp, normed, t.units(2, 2))
                h, b = t.head_batch()
                sp.dma_start(a["heads"][h * B + b, :, :], head[t.side][:, :]).then_inc(head_out[t.side], 16)

            def step(r, t):
                w = Tile(r, t + LEAD)
                if w.real():
                    if w.i == 0 and Tile(r, t + LEAD + TILES).real():
                        load_qv(Tile(r, t + LEAD + TILES))
                    write(w)
                back = Tile(r, t + LEAD - READ_LAG)
                if back.real():
                    read_back(back)
                if t % TILES == 1 and Tile(r, t - 1 + TILES).real():
                    load_qk(Tile(r, t - 1 + TILES))
                done = Tile(r, t - TILES)
                if t % TILES == 3 and done.real():
                    store_head(done)

            for g, k in enumerate(RIGHT_PARTS):
                sp.dma_start(pos_keys[DH * g:DH * (g + 1), :, :],
                             a["pos_parts"][k].rearrange("(h d) m -> d h m", d=DH)).then_inc(packed, 16)
            load_qv(Tile(0, 0))
            load_qv(Tile(0, TILES))
            load_qk(Tile(0, 0))
            for w in range(LEAD):
                write(Tile(0, w))
                if w >= READ_LAG:
                    read_back(Tile(0, w - READ_LAG))
            rounds(sp, step)
            for k in range(2):
                sp.wait_ge(head_out[k], 16 * UNITS // 2)

        @block.tensor
        def _(pe):
            def positional(t):
                pos_head, _ = t.head_batch()
                if t.i == 0:
                    pe.wait_ge(qv_in[t.side], t.r * 48 + (t.unit_in_body // 2 + 1) * 48)
                if t.past(1):
                    pe.wait_ge(pos_copied, t.count())
                for n in range(2):
                    ins = pe.matmul(ps_pos[:, n, :], q_v[t.side][:, t.i * P:(t.i + 1) * P],
                                    pos_keys[:, bass.ds(pos_head, 1), n * 512:(n + 1) * 512]
                                    .rearrange("p a m -> p (a m)"), start=True, stop=True)
                ins.then_inc(pos_mm, 1)

            def content(t):
                if t.i == 0:
                    pe.wait_ge(qk_in[t.side], t.r * 96 + (t.unit_in_body // 2 + 1) * 96)
                if t.past(1):
                    pe.wait_ge(scored, t.count())
                for n in range(2):
                    ins = pe.matmul(ps_con[:, n, :], q_u[t.side][:, t.i * P:(t.i + 1) * P],
                                    keys[t.side][:, n * 512:(n + 1) * 512], start=True, stop=True)
                ins.then_inc(con_mm, 1)

            def turn(t):
                pe.wait_ge(shifted, t.count(1, 1))
                for n in range(2):
                    if t.past(1):
                        pe.wait_ge(exped, t.count(2, n - 1))
                    for j in range(4):
                        kt = 4 * n + j
                        ins = pe.transpose(ps_turn[:, n, j * P:(j + 1) * P],
                                           score[:, t.slot, kt * P:(kt + 1) * P], keep["ident"][:, :])
                    ins.then_inc(turned, 1)

            def times_values(t):
                pe.wait_ge(v_ready, t.units(1, 1))
                pe.wait_ge(exped, t.count(2, 2 * QUAD))
                if t.past(QUAD):
                    pe.wait_ge(pv_copied, t.quads())
                for kt in range(TILES):
                    g = kt % 4
                    ins = pe.matmul(ps_pv[VW * g:VW * (g + 1), :], v_aug[t.side][:, kt, :],
                                    prob[t.t // QUAD % 2][:, kt, :], start=(kt < 4), stop=(kt >= 4))
                ins.then_inc(pv_mm, 1)

            def fold(t):
                pe.wait_ge(pv_copied, t.quads(1))
                if t.past(QUAD):
                    pe.wait_ge(normed, t.quads())
                for k in range(QUAD):
                    ins = pe.matmul(ps_head[:, k, 0:VW], head_T[:, k * P:(k + 1) * P], keep["fold"][:, :],
                                    start=True, stop=True)
                ins.then_inc(head_mm, 1)

            def step(r, t):
                if t % QUAD == 3 and Tile(r, t - 7).real():
                    fold(Tile(r, t - 7))
                if Tile(r, t + LEAD).real():
                    positional(Tile(r, t + LEAD))
                if Tile(r, t).real():
                    content(Tile(r, t))
                if t % QUAD == 1 and Tile(r, t - 5).real():
                    times_values(Tile(r, t - 5))
                if Tile(r, t - 1).real():
                    turn(Tile(r, t - 1))

            pe.wait_ge(packed, 16 * len(RIGHT_PARTS))
            pe.wait_ge(cleared, 1)
            for t in range(LEAD):
                positional(Tile(0, t))
            rounds(pe, step)

        @block.scalar
        def _(act):
            def copy_positional(t):
                act.wait_ge(pos_mm, t.count(1, 1))
                if t.past(RING):
                    act.wait_ge(written[t.slot], t.rounds(RING))
                act.activation(pos_out[:, t.slot, :], ps_pos[:, :, :].rearrange("p a m -> p (a m)"), ACT.Copy)\
                    .then_inc(pos_copied, 1)

            def exponentials(t):
                if t.i % QUAD == 0 and t.past(2 * QUAD):
                    act.wait_ge(pv_mm, t.quads(-1))
                for n in range(2):
                    act.wait_ge(turned, t.count(2, n + 1))
                    k = t.t % QUAD
                    act.activation(prob[t.t // QUAD % 2][:, 4 * n:4 * n + 4, k * P:(k + 1) * P],
                                   ps_turn[:, n, :].rearrange("p (j i) -> p j i", i=P), ACT.Exp)\
                        .then_inc(exped, 1)

            def step(r, t):
                if Tile(r, t + LEAD).real():
                    copy_positional(Tile(r, t + LEAD))
                if Tile(r, t - 1).real():
                    exponentials(Tile(r, t - 1))

            for t in range(LEAD):
                copy_positional(Tile(0, t))
            rounds(act, step)

        @block.vector
        def _(dve):
            def total(t):
                dve.wait_ge(con_mm, t.count(1, 1))
                dve.wait_ge(read[t.slot], t.rounds(RING, 1))
                if t.past(RING):
                    dve.wait_ge(turned, t.count(2, 2 - 2 * RING))
                dve.nop(nofuse=True)
                dve.tensor_tensor_reduce(score[:, t.slot, :], ps_con[:, :, :].rearrange("p a m -> p (a m)"),
                                         pos_in[:, t.slot, :], SCALE, -3.0e38, ALU.add, ALU.max,
                                         row_max[:, t.slot:t.slot + 1]).then_inc(scored, 1)
                dve.wait_ge(scored, t.count(1, 1))
                dve.tensor_scalar(neg_max[:, t.slot:t.slot + 1], row_max[:, t.slot:t.slot + 1], -1.0, None,
                                  ALU.mult).then_inc(negated, 1)

            def copy_products(t):
                dve.wait_ge(pv_mm, t.quads(1))
                if t.past(QUAD):
                    dve.wait_ge(head_mm, t.quads())
                dve.tensor_copy(head_T[:, :], ps_pv[:, :]).then_inc(pv_copied, 1)

            def normalise(t):
                dve.wait_ge(head_mm, t.quads(1))
                if t.past(QUAD):
                    dve.wait_ge(normed, t.quads())
                dve.reciprocal(inverse[:, :], ps_head[:, :, DH]).then_inc(inverted, 1)
                dve.wait_ge(inverted, t.quads(1))
                if t.i == 0 and t.past(BODY):
                    dve.wait_ge(head_out[t.side], t.r * 16 + 16 * (t.unit_in_body // 2))
                q = t.i // QUAD
                dve.tensor_tensor(head[t.side][:, :].rearrange("p (t d) -> p t d", d=DH)[:, QUAD * q:QUAD * (q + 1), :],
                                  ps_head[:, :, 0:DH], inverse[:, :].unsqueeze(2).to_broadcast([P, QUAD, DH]),
                                  ALU.mult).then_inc(normed, 1)

            def step(r, t):
                if Tile(r, t).real():
                    total(Tile(r, t))
                if t % QUAD == 2 and Tile(r, t - 6).real():
                    copy_products(Tile(r, t - 6))
                if t % QUAD == 3 and Tile(r, t - 7).real():
                    normalise(Tile(r, t - 7))

            rounds(dve, step)

        @block.gpsimd
        def _(pool):
            def less_maximum(t):
                at_once(pool, negated, t.count(1, 1))
                pool.tensor_scalar(score[:, t.slot, :], score[:, t.slot, :], neg_max[:, t.slot:t.slot + 1], 1.0,
                                   ALU.add, ALU.mult).then_inc(shifted, 1)

            def copy_values(t):
                pool.wait_ge(vals_in[t.side], t.r * 16 + 16 * (t.unit_in_body // 2 + 1))
                if t.past(BODY):
                    pool.wait_ge(pv_mm, t.units(2, -2))
                pool.nop(nofuse=True)
                pool.tensor_copy(v_aug[t.side][:, :, 0:DH], v_in[t.side][:, :].rearrange("p (j d) -> p j d", d=DH))\
                    .then_inc(v_ready, 1)

            def step(r, t):
                if Tile(r, t).real():
                    less_maximum(Tile(r, t))
                    if t % TILES == 0:
                        copy_values(Tile(r, t))

            for k in range(2):
                pool.memset(v_aug[k][:, :, DH:DH + 1], 1.0)
                ins = pool.memset(v_aug[k][:, :, DH + 1:VW], 0.0)
            ins.then_inc(cleared, 1)
            rounds(pool, step)


def closing_phase(nc, keep, a):
    with ExitStack() as ctx:
        def pair(name, shape, dt=F32):
            return [ctx.enter_context(nc.sbuf_tensor(f"cl_{name}{k}", shape, dt)) for k in range(2)]

        def sem(name):
            return ctx.enter_context(nc.semaphore("cl_" + name))

        heads = pair("heads", [P, H, GROUP * DH])
        x1_bo, x2, z, act_in, out, by_row = (
            pair(n, [P, GROUP, D]) for n in ("x1_bo", "x2", "z", "act_in", "out", "by_row"))
        head_T, zT = pair("head_T", [P, C, ROWS]), pair("zT", [P, C, ROWS])
        stats, moments = pair("stats", [P, GROUP, 6]), pair("moments", [P, GROUP, 2])
        scale, variance = pair("scale", [P, GROUP]), pair("variance", [P, GROUP])
        ps = [ctx.enter_context(nc.psum_tensor(f"cl_ps{k}", [P, 4, 512], F32)) for k in range(2)]
        heads_in, x1_in, out_done = ([sem(f"{n}{k}") for k in range(2)] for n in ("heads_in", "x1_in", "out_done"))
        ln = [sem("ln_" + n) for n in ("stats", "moments", "variance", "scale", "out")]
        regrouped, turned1, headT, proj, x2_ready, turned2, zT_ready, ffn, biased, tanhed, out_ready = (
            sem(n) for n in ("regrouped", "turned1", "headT", "proj", "x2_ready", "turned2", "zT_ready", "ffn", "biased",
                             "tanhed", "out_ready"))
        x1_rows = a["x1"].rearrange("(g t p) d -> p g t d", p=P, t=GROUP)
        out_rows = a["out"].rearrange("b (g t p) d -> p (b g) t d", p=P, t=GROUP)
        head_rows = a["heads"].rearrange("(h b) p n -> b p h n", b=B)
        block = ctx.enter_context(nc.Block())

        @block.sync
        def _(sp):
            def load_heads(b, k):
                w = GROUP * DH
                sp.dma_start(heads[k][:, :, :], head_rows[b, :, :, k * w:(k + 1) * w]).then_inc(heads_in[k], 16)

            def load_x1(b, k):
                sp.dma_start(x1_bo[k][:, :, :], x1_rows[:, b * 2 + k, :, :]).then_inc(x1_in[k], 16)

            def step(b, c):
                if b is not None:
                    for k in range(2):
                        if c is not None:
                            sp.wait_ge(regrouped, b * 2 + (k - 1))
                        load_heads(b, k)
                    for k in range(2):
                        if c is not None:
                            sp.wait_ge(x2_ready, b * 2 + (k - 1))
                        load_x1(b, k)
                if c is not None:
                    for k in range(2):
                        sp.wait_ge(out_ready, c * 2 + (k + 1))
                        sp.dma_start(out_rows[:, c * 2 + k, :, :], out[k][:, :, :]).then_inc(out_done[k], 16)

            over_rounds(sp, step)
            for k in range(2):
                sp.wait_ge(out_done[k], 16 * B)

        @block.tensor
        def _(pe):
            def step(b, c):
                if c is not None:
                    for k in range(2):
                        pe.wait_ge(ln[4], c * 2 + (k + 1))
                        turn_rows(pe, ps[k], lambda t, f: z[k][:, t, f * P:(f + 1) * P], keep["ident"])\
                            .then_inc(turned2, 1)
                    for k in range(2):
                        pe.wait_ge(zT_ready, c * 2 + (k + 1))
                        rows_times(pe, ps[k][:, 2:4, :], zT[k], keep["w3"]).then_inc(ffn, 1)
                if b is not None:
                    for k in range(2):
                        pe.wait_ge(regrouped, b * 2 + (k + 1))
                        turn_rows(pe, ps[k], lambda t, f: by_row[k][:, t, f * P:(f + 1) * P], keep["ident"])\
                            .then_inc(turned1, 1)
                    for k in range(2):
                        pe.wait_ge(headT, b * 2 + (k + 1))
                        if c is not None:
                            pe.wait_ge(biased, c * 2 + (k + 1))
                        rows_times(pe, ps[k][:, 2:4, :], head_T[k], keep["wo"]).then_inc(proj, 1)

            over_rounds(pe, step)

        @block.scalar
        def _(act):
            def step(b, c):
                if c is not None:
                    for k in range(2):
                        act.wait_ge(turned2, c * 2 + (k + 1))
                        act.activation(zT[k][:, :, :], ps[k][:, 0:2, :], ACT.Copy).then_inc(zT_ready, 1)
                if b is not None:
                    for k in range(2):
                        act.wait_ge(heads_in[k], b * 16 + 16)
                        reused(act, turned1, b * 2)
                        act.activation(by_row[k][:, :, :].rearrange("p t (h d) -> p t h d", d=DH),
                                       heads[k][:, :, :].rearrange("p h (t d) -> p t h d", d=DH), ACT.Copy)\
                            .then_inc(regrouped, 1)
                    for k in range(2):
                        act.wait_ge(turned1, b * 2 + (k + 1))
                        act.activation(head_T[k][:, :, :], ps[k][:, 0:2, :], ACT.Copy).then_inc(headT, 1)
                if c is not None:
                    for k in range(2):
                        act.wait_ge(biased, c * 2 + (k + 1))
                        act.activation(act_in[k][:, :, :], act_in[k][:, :, :], ACT.Tanh).then_inc(tanhed, 1)

            over_rounds(act, step)

        @block.vector
        def _(dve):
            def step(b, c):
                if c is not None:
                    for k in range(2):
                        dve.wait_ge(ffn, c * 2 + (k + 1))
                        dve.tensor_tensor(act_in[k][:, :, :],
                                          ps[k][:, 2:4, :].rearrange("p a (t d) -> p (a t) d", d=D),
                                          broadcast_groups(keep["b_ffn"][:, :]), ALU.add).then_inc(biased, 1)
                    for k in range(2):
                        dve.wait_ge(tanhed, c * 2 + (k + 1))
                        reused(dve, out_done[k], c * 16)
                        dve.scalar_tensor_tensor(out[k][:, :, :].rearrange("p t d -> p (t d)"),
                                                 act_in[k][:, :, :].rearrange("p t d -> p (t d)"), 0.5,
                                                 x2[k][:, :, :].rearrange("p t d -> p (t d)"), ALU.mult, ALU.add)\
                            .then_inc(out_ready, 1)
                if b is not None:
                    for k in range(2):
                        g = b * 2 + k
                        dve.wait_ge(proj, g + 1)
                        dve.wait_ge(x1_in[k], b * 16 + 16)
                        reused(dve, out_ready, b * 2)
                        dve.tensor_tensor(x2[k][:, :, :], ps[k][:, 2:4, :].rearrange("p a (t d) -> p (a t) d", d=D),
                                          x1_bo[k][:, :, :], ALU.add).then_inc(x2_ready, 1)
                        dve.wait_ge(x2_ready, g + 1)
                        layer_norm(dve, x2[k], stats[k], moments[k], variance[k][:, :], scale[k][:, :], ln, g, z[k],
                                   False)

            over_rounds(dve, step)

        @block.gpsimd
        def _(pool):
            def step(b, c):
                if b is not None:
                    for k in range(2):
                        inverse_root(pool, keep, variance[k][:, :], scale[k][:, :], ln, b * 2 + k)

            over_rounds(pool, step)


def macaron_layer(nc, a):
    def scratch(name, shape, dt=F32):
        a[name] = nc.dram_tensor("scratch_" + name, shape, dt, kind="Internal").ap()

    scratch("scores", [2, S * PITCH])
    scratch("pos_parts", [3, D, S], BF16)
    scratch("qk_parts", [3, 3, B, D, S], BF16)
    scratch("values", [UNITS, P, P])
    scratch("heads", [UNITS, P, P])
    scratch("x1", [B * S, D])
    with ExitStack() as ctx:
        def sb(name, shape, dt=F32):
            return ctx.enter_context(nc.sbuf_tensor("keep_" + name, shape, dt))

        keep = {n: sb(n, [P, C, D]) for n in ("wq", "wk", "wv", "wo", "w3")}
        keep |= {n: sb(n, [P, D]) for n in ("b_ffn", "bo", "bv")}
        keep["b_qk"] = sb("b_qk", [P, 3, C])
        keep["minus_half"] = sb("minus_half", [P, GROUP])
        keep["ident"] = sb("ident", [P, P])
        keep["fold"] = sb("fold", [P, VW])
        setup_phase(nc, keep, a)
        dense_phase(nc, keep, a)
        attention_phase(nc, keep, a)
        closing_phase(nc, keep, a)


_INS = ['L0_attn_x', 'L0_attn_ln_g', 'L0_attn_ln_b', 'L0_attn_Wq', 'L0_attn_bq', 'L0_attn_Wk', 'L0_attn_bk',
        'L0_attn_Wv', 'L0_attn_bv', 'L0_attn_Wp', 'L0_attn_Wo', 'L0_attn_bo', 'L0_attn_u_bias', 'L0_attn_v_bias',
        'L0_ffn_weight', 'L0_ffn_aux_weight1', 'L0_ffn_aux_weight2', 'L0_ffn_bias']


def constants():
    import math
    import numpy as np
    pos = np.arange(S, dtype=np.float32)[:, None]
    div = np.exp(np.arange(0, D, 2, dtype=np.float32) * np.float32(-math.log(10000.0) / D))
    ang = pos * div
    pe = np.stack([np.sin(ang), np.cos(ang)], axis=-1).reshape(S, D)
    return {"pe_T": np.ascontiguousarray(pe.T, dtype=np.float32), "ident": np.eye(P, dtype=np.float32),
            "fold": np.tile(np.eye(VW, dtype=np.float32), (P // VW, 1))}


def kernel(**inputs):
    import numpy as _np
    import concourse.bacc as _bacc
    from concourse import mybir as _mybir
    from concourse.bass_utils import run_bass_kernel_spmd as _run

    nc = _bacc.Bacc("TRN2", target_bir_lowering=False, num_devices=1)
    arrays, args = {}, {}
    given = {n: _np.ascontiguousarray(inputs[n]) for n in _INS} | constants()
    for name, x in given.items():
        arrays[f"in_{name}_dram"] = x
        args[name] = nc.dram_tensor(f"in_{name}_dram", x.shape, _mybir.dt.from_np(x.dtype), kind="ExternalInput").ap()
    args["out"] = nc.dram_tensor("out_0_dram", [B, S, D], F32, kind="ExternalOutput").ap()
    macaron_layer(nc, args)
    r = _run(nc, [arrays], core_ids=[0])
    return r.results[0]["out_0_dram"]
```
